# Optimizing a Trainium2 kernel written in Bass

```python
import numpy as np
import jax
import jax.numpy as jnp

def _softmax(x, axis=-1):
    return jax.nn.softmax(x, axis=axis)

def _gelu(x):
    return jax.nn.gelu(x, approximate=True)

def _silu(x):
    return jax.nn.silu(x)

def _sigmoid(x):
    return jax.nn.sigmoid(x)

def _layernorm(x, axis=-1, eps=1e-05):
    m = jnp.mean(x, axis=axis, keepdims=True)
    v = jnp.var(x, axis=axis, keepdims=True)
    return (x - m) / jnp.sqrt(v + eps)

def _scatter_add(tgt, idx, src, axis=0):
    return tgt.at[idx].add(src)

def _segment_sum(src, seg, n):
    return jax.ops.segment_sum(src, seg, n)
kernel_name = 'mk_hybrid_d1_jaxref_r8_71bbf6'

def setup_inputs(seed: int=0):
    np.random.seed(seed)
    _w = jnp.asarray

    def _L0_attn_a_setup():
        import jax, jax.numpy as jnp
        import numpy as np
        D_ATT_IN = 128
        NUM_HEADS = 16
        D_Q = 64
        D_V = 64
        D_MODEL = 128

        def _trunc_normal(key, shape, std):
            return jax.random.truncated_normal(key, -3.0, 3.0, shape, dtype=jnp.float32) * std
        key = jax.random.key(seed)
        k_x, k_q, k_k, k_v, k_o = jax.random.split(key, 5)

        def init_w(k, out_f, in_f):
            s = np.sqrt(2.0 / (in_f + out_f))
            return _trunc_normal(k, (out_f, in_f), s)
        return {'in_features': jax.random.normal(k_x, (4, 256, D_ATT_IN), dtype=jnp.float32), 'w_q': init_w(k_q, NUM_HEADS * D_Q, D_ATT_IN), 'w_k': init_w(k_k, NUM_HEADS * D_Q, D_ATT_IN), 'w_v': init_w(k_v, NUM_HEADS * D_V, D_ATT_IN), 'w_o': init_w(k_o, D_MODEL, NUM_HEADS * D_V)}
    _L0_attn_a_in = _L0_attn_a_setup()

    def _L0_attn_b_setup():
        import jax, jax.numpy as jnp
        import numpy as np
        N_EMBD = 128
        N_HEAD = 16
        HEAD_SIZE = 64
        LN_EPS = 0.001
        key = jax.random.key(seed)
        ks = jax.random.split(key, 7)
        B, S, D, H, E = (4, 256, N_EMBD, N_HEAD, HEAD_SIZE)
        x = jax.random.normal(ks[0], (B, S, D), dtype=jnp.float32)
        scale = 1.0 / np.sqrt(D)
        Wq = jax.random.normal(ks[1], (H, D, E), dtype=jnp.float32) * scale
        Wk = jax.random.normal(ks[2], (H, D, E), dtype=jnp.float32) * scale
        Wv = jax.random.normal(ks[3], (H, D, E), dtype=jnp.float32) * scale
        Wo = jax.random.normal(ks[4], (H * E, D), dtype=jnp.float32) * scale
        gamma = jnp.ones((D,), dtype=jnp.float32)
        beta = jnp.zeros((D,), dtype=jnp.float32)
        return {'x': x, 'Wq': Wq, 'Wk': Wk, 'Wv': Wv, 'Wo': Wo, 'gamma': gamma, 'beta': beta}
    _L0_attn_b_in = _L0_attn_b_setup()

    def _L0_ffn_setup():
        import jax, jax.numpy as jnp
        import numpy as np
        D_MODEL = 128
        M = 64
        INNER = 16
        key = jax.random.key(seed)
        ks = jax.random.split(key, 9)

        def init(k, shape, fan_in):
            bound = 1.0 / np.sqrt(fan_in)
            return jax.random.uniform(k, shape, jnp.float32, -bound, bound)
        x = jax.random.normal(ks[0], (16, 512, D_MODEL), dtype=jnp.float32)
        Win = init(ks[1], (D_MODEL, M), D_MODEL)
        bin_ = init(ks[2], (M,), D_MODEL)
        W1 = init(ks[3], (M, INNER), 1)
        b1 = init(ks[4], (M, INNER), 1)
        W2 = init(ks[5], (M, INNER), INNER)
        b2 = init(ks[6], (M,), INNER)
        Wout = init(ks[7], (M, D_MODEL), M)
        bout = init(ks[8], (D_MODEL,), M)
        return {'x': x, 'Win': Win, 'bin_': bin_, 'W1': W1, 'b1': b1, 'W2': W2, 'b2': b2, 'Wout': Wout, 'bout': bout}
    _L0_ffn_in = _L0_ffn_setup()
    _d = {'L0_attn_a_in_features': _L0_attn_a_in['in_features'], 'L0_attn_a_w_q': _L0_attn_a_in['w_q'], 'L0_attn_a_w_k': _L0_attn_a_in['w_k'], 'L0_attn_a_w_v': _L0_attn_a_in['w_v'], 'L0_attn_a_w_o': _L0_attn_a_in['w_o'], 'L0_attn_b_Wq': _L0_attn_b_in['Wq'], 'L0_attn_b_Wk': _L0_attn_b_in['Wk'], 'L0_attn_b_Wv': _L0_attn_b_in['Wv'], 'L0_attn_b_Wo': _L0_attn_b_in['Wo'], 'L0_attn_b_gamma': _L0_attn_b_in['gamma'], 'L0_attn_b_beta': _L0_attn_b_in['beta'], 'L0_ffn_Win': _L0_ffn_in['Win'], 'L0_ffn_bin_': _L0_ffn_in['bin_'], 'L0_ffn_W1': _L0_ffn_in['W1'], 'L0_ffn_b1': _L0_ffn_in['b1'], 'L0_ffn_W2': _L0_ffn_in['W2'], 'L0_ffn_b2': _L0_ffn_in['b2'], 'L0_ffn_Wout': _L0_ffn_in['Wout'], 'L0_ffn_bout': _L0_ffn_in['bout']}
    _x0 = _d['L0_attn_a_in_features']
    _d['L0_attn_a_in_features'] = jax.random.normal(jax.random.fold_in(jax.random.key(seed), 1), (8, 512, 128), dtype=_x0.dtype)
    del _x0
    return _d

def reference(L0_attn_a_in_features, L0_attn_a_w_q, L0_attn_a_w_k, L0_attn_a_w_v, L0_attn_a_w_o, L0_attn_b_Wq, L0_attn_b_Wk, L0_attn_b_Wv, L0_attn_b_Wo, L0_attn_b_gamma, L0_attn_b_beta, L0_ffn_Win, L0_ffn_bin_, L0_ffn_W1, L0_ffn_b1, L0_ffn_W2, L0_ffn_b2, L0_ffn_Wout, L0_ffn_bout):

    def _L0_attn_a_ref(in_features, w_q, w_k, w_v, w_o):
        import jax, jax.numpy as jnp
        import numpy as np
        D_ATT_IN = 128
        NUM_HEADS = 16
        D_Q = 64
        D_V = 64
        D_MODEL = 128

        def _trunc_normal(key, shape, std):
            return jax.random.truncated_normal(key, -3.0, 3.0, shape, dtype=jnp.float32) * std
        q = jnp.einsum('oi,bsi->bso', w_q, in_features)
        k = jnp.einsum('oi,bsi->bso', w_k, in_features)
        v = jnp.einsum('oi,bsi->bso', w_v, in_features)
        s = in_features.shape[-2]
        scores = jnp.einsum('bqd,bkd->bqk', q, k) / jnp.sqrt(jnp.asarray(k.shape[-1], q.dtype))
        causal = jnp.tril(jnp.ones((s, s), dtype=bool))
        scores = jnp.where(causal[None, :, :], scores, -jnp.inf)
        att = jax.nn.softmax(scores, axis=-1)
        ctx = jnp.einsum('bqk,bkd->bqd', att, v)
        return jnp.einsum('oi,bsi->bso', w_o, ctx)

    def _L0_attn_b_ref(x, Wq, Wk, Wv, Wo, gamma, beta):
        import jax, jax.numpy as jnp
        import numpy as np
        N_EMBD = 128
        N_HEAD = 16
        HEAD_SIZE = 64
        LN_EPS = 0.001
        B, S, D = x.shape
        H, _, E = Wq.shape
        q = jnp.einsum('bsd,hde->bhse', x, Wq)
        k = jnp.einsum('bsd,hde->bhse', x, Wk)
        v = jnp.einsum('bsd,hde->bhse', x, Wv)
        scores = jnp.einsum('bhse,bhte->bhst', q, k)
        causal = jnp.tril(jnp.ones((S, S), dtype=bool))
        scores = jnp.where(causal, scores / jnp.sqrt(jnp.float32(E)), jnp.float32(-jnp.inf))
        attn = jax.nn.softmax(scores, axis=-1)
        out = jnp.einsum('bhst,bhte->bhse', attn, v)
        heads = out.transpose(0, 2, 1, 3).reshape(B, S, H * E)
        y = x + heads @ Wo
        mu = jnp.mean(y, axis=-1, keepdims=True)
        var = jnp.mean(jnp.square(y - mu), axis=-1, keepdims=True)
        y = (y - mu) * jax.lax.rsqrt(var + LN_EPS) * gamma + beta
        return y

    def _L0_ffn_ref(x, Win, bin_, W1, b1, W2, b2, Wout, bout):
        import jax, jax.numpy as jnp
        import numpy as np
        D_MODEL = 128
        M = 64
        INNER = 16
        s = jnp.einsum('btd,dm->btm', x, Win) + bin_
        h = jax.nn.relu(s[..., None] * W1 + b1)
        g = jnp.einsum('btmh,mh->btm', h, W2) + b2
        out = jnp.einsum('btm,md->btd', g, Wout) + bout
        return out
    x = L0_attn_a_in_features
    x = x + _L0_attn_a_ref(_layernorm(x, axis=-1), L0_attn_a_w_q, L0_attn_a_w_k, L0_attn_a_w_v, L0_attn_a_w_o)
    x = x + _L0_ffn_ref(_layernorm(x, axis=-1), L0_ffn_Win, L0_ffn_bin_, L0_ffn_W1, L0_ffn_b1, L0_ffn_W2, L0_ffn_b2, L0_ffn_Wout, L0_ffn_bout)
    x = x + _L0_attn_b_ref(_layernorm(x, axis=-1), L0_attn_b_Wq, L0_attn_b_Wk, L0_attn_b_Wv, L0_attn_b_Wo, L0_attn_b_gamma, L0_attn_b_beta)
    x = x + _L0_ffn_ref(_layernorm(x, axis=-1), L0_ffn_Win, L0_ffn_bin_, L0_ffn_W1, L0_ffn_b1, L0_ffn_W2, L0_ffn_b2, L0_ffn_Wout, L0_ffn_bout)
    return x

_drawn_inputs = setup_inputs


def setup_inputs(seed=0):
    import zlib

    import numpy as np

    out = dict(_drawn_inputs(seed))
    spreads = {'L0_attn_b_gamma': (1.0, 0.2), 'L0_attn_b_beta': (0.0, 0.1)}
    factors = {'L0_attn_a_w_q': 3.228, 'L0_attn_a_w_k': 3.125, 'L0_ffn_bin_': 5.196}
    for name, (base, spread) in spreads.items():
        noise = np.random.default_rng([zlib.crc32(name.encode()), seed]).standard_normal(out[name].shape)
        drawn = base * np.exp(spread * noise) if base else spread * noise
        out[name] = jnp.asarray(drawn.astype(out[name].dtype))
    for name, factor in factors.items():
        out[name] = (out[name] * factor).astype(out[name].dtype)
    return out
```

```python
from contextlib import ExitStack

import concourse.bass as bass
from concourse import mybir

F32 = mybir.dt.float32
F32R = mybir.dt.float32r
F16 = mybir.dt.float16
BF16 = mybir.dt.bfloat16
ALU = mybir.AluOpType
ACT = mybir.ActivationFunctionType
AX = mybir.AxisListType

P = 128
MASKED = -3.0e38
LN_EPS = 1e-5
LN_B_EPS = 1e-3
TINY = 1e-30

UNIT_ROWS = [(0, 1), (2,), (3,)]
NU = len(UNIT_ROWS)
SCORE_AT = {0: 0, 1: 256, 2: 0, 3: 0}
SCORE_N = {0: 256, 1: 256, 2: 384, 3: 512}


def unit_blocks(u):
    return [(i, j) for i in UNIT_ROWS[u] for j in range(i + 1)]


def hybrid_kernel(nc, x_in, a_wq, a_wk, a_wv, a_wo, b_wq, b_wk, b_wv, b_wo, gamma, beta,
                  f_win, f_bin, f_w1, f_b1, f_w2, f_b2, f_wout, f_bout, out):
    B, S, D = x_in.shape
    H, _, E = b_wq.shape
    O = a_wq.shape[0]
    M, INNER = f_w1.shape
    QB = S // P
    NT = B * QB
    OC = O // P
    HP = H // 2
    PAIRS = B * HP
    J = INNER // 2
    SLOTS = 2 * HP
    assert D == P and S == 4 * P and 2 * E == P and 2 * M == P and H * E == O

    with ExitStack() as ctx:
        def sb(name, shape, dt=F32):
            return ctx.enter_context(nc.sbuf_tensor(name, shape, dt))

        sems = {}

        def sem(name):
            if name not in sems:
                sems[name] = ctx.enter_context(nc.semaphore(name))
            return sems[name]

        def wait(eng, name, count):
            if isinstance(count, int) and count <= 0:
                return
            eng.wait_ge(sem(name), count)

        bank = [ctx.enter_context(nc.psum_tensor(f"bank{i}", [P, 512], F32)) for i in range(8)]

        ident = sb("ident", [P, P])
        ident_bf = sb("ident_bf", [P, P], BF16)
        mask_bf = sb("mask_bf", [P, P], BF16)
        rs_power = sb("rs_power", [P, QB])
        minus_one = sb("minus_one", [P, QB])
        ln_eps = sb("ln_eps", [P, QB])
        ln_b_eps = sb("ln_b_eps", [P, QB])
        gamma_sb = sb("gamma_sb", [P, P])
        beta_sb = sb("beta_sb", [P, P])
        bout_sb = sb("bout_sb", [P, P])
        win2 = sb("win2", [P, 2, M])
        wout2 = sb("wout2", [P, P])
        w1_2 = sb("w1_2", [P, J])
        b1_2 = sb("b1_2", [P, J])
        w2_2 = sb("w2_2", [P, J])
        b2_2 = sb("b2_2", [P, 1])
        bin_2 = sb("bin_2", [P, 1])

        qk_a = sb("qk_a", [P, P])
        qk_a_hi = sb("qk_a_hi", [P, P], F32R)
        qk_a_lo = sb("qk_a_lo", [P, P], F32R)
        vo_a = sb("vo_a", [P, P])
        qk_b_parts = sb("qk_b_parts", [P, H, 2, P], F32R)
        wv_b_hi = sb("wv_b_hi", [P, O], F32R)
        wv_b_lo = sb("wv_b_lo", [P, O], F32R)
        wo_b_parts = sb("wo_b_parts", [P, HP, 2, P], F32R)
        win_hi = sb("win_hi", [P, P], F32R)
        win_lo = sb("win_lo", [P, P], F32R)
        largest = sb("largest", [P, 2])
        largest_all = sb("largest_all", [P, 2])
        scale_up = sb("scale_up", [P, 2])
        scale_down = sb("scale_down", [P, 2])

        x_sb = sb("x_sb", [P, NT, P])
        yt = sb("yt", [P, B * S])
        xt_hi = sb("xt_hi", [P, B * S], F32R)
        xt_lo = sb("xt_lo", [P, B * S], F32R)

        prob = [sb(f"prob{u}", [P, 512]) for u in range(NU)]
        prob_t_hi = [sb(f"prob_t_hi{u}", [P, 512], F16) for u in range(NU)]
        prob_t_lo = [sb(f"prob_t_lo{u}", [P, 512], F16) for u in range(NU)]

        def split_product(pe, dst, lhs_hi, lhs_lo, rhs_hi, rhs_lo, start=True, stop=True):
            pe.matmul(dst, lhs_hi, rhs_hi, start=start, stop=False)
            pe.matmul(dst, lhs_hi, rhs_lo, start=False, stop=False)
            return pe.matmul(dst, lhs_lo, rhs_hi, start=False, stop=stop)

        def scores(pe, dst, u, g_hi, g_lo, x_hi, x_lo, at):
            for i in UNIT_ROWS[u]:
                c, n = SCORE_AT[i], SCORE_N[i]
                split_product(pe, dst[:, c:c + n], g_hi[:, i * P:(i + 1) * P], g_lo[:, i * P:(i + 1) * P],
                              x_hi[:, bass.ds(at, n)], x_lo[:, bass.ds(at, n)], stop=False)
                last = pe.matmul(dst[:, c + i * P:c + (i + 1) * P], ident_bf[:, :], mask_bf[:, :],
                                 start=False, stop=True)
            return last

        def row_maxima(dve, src, u, neg_max):
            for i in UNIT_ROWS[u]:
                c = SCORE_AT[i]
                last = dve.tensor_reduce(neg_max[:, i:i + 1], src[:, c:c + (i + 1) * P], AX.X, ALU.max,
                                         negate=True)
            return last

        def exponentials(act, src, u, neg_max, sums):
            at = 0
            for i in UNIT_ROWS[u]:
                c, n = SCORE_AT[i], (i + 1) * P
                last = act.activation(prob[u][:, at:at + n], src[:, c:c + n], ACT.Exp,
                                      bias=neg_max[:, i:i + 1], accum_out=sums[:, i:i + 1])
                at += n
            return last

        def transposes(pe, dst, src, n):
            for k in range(n):
                last = pe.transpose(dst[:, k * P:(k + 1) * P], src[:, k * P:(k + 1) * P], ident[:, :])
            return last

        def weighted_values(pe, dst, u, v_hi, v_lo):
            k = 0
            for i, j in unit_blocks(u):
                blk = slice(k * P, (k + 1) * P)
                pe.matmul(dst(i), prob_t_hi[u][:, blk], v_hi(j), start=(j == 0), stop=False)
                pe.matmul(dst(i), prob_t_hi[u][:, blk], v_lo(j), start=False, stop=False)
                last = pe.matmul(dst(i), prob_t_lo[u][:, blk], v_hi(j), start=False, stop=(j == i))
                k += 1
            return last


        def prepare_loads_scalar(act):
            for dst, src in a_loads:
                act.dma_start(dst, src).then_inc(sem(LOADED_A), 16)

        def prepare_loads_sync(sp):
            for dst, src in b_loads:
                sp.dma_start(dst, src).then_inc(sem(LOADED_B), 16)
            sp.wait_ge(sem("b2_zeroed"), 1)
            for dst, src in f_loads:
                sp.dma_start(dst, src).then_inc(sem(LOADED_F), 16)

        def prepare_gpsimd(pool):
            pool.memset(ident[:, :], 0.0).then_inc(sem("const_0"), 1)
            pool.memset(ident_bf[:, :], 0.0).then_inc(sem("const_0"), 1)
            pool.memset(mask_bf[:, :], 0.0).then_inc(sem("const_0"), 1)
            for m, value in ((rs_power, -0.5), (minus_one, -1.0), (ln_eps, LN_EPS), (ln_b_eps, LN_B_EPS)):
                pool.memset(m[:, :], value).then_inc(sem("const_0"), 1)
            pool.memset(b2_2[:, :], 0.0).then_inc(sem("b2_zeroed"), 1)
            pool.wait_ge(sem("const_0"), 7)
            for m in (ident, ident_bf):
                pool.affine_select(out=m[:, :], in_=m[:, :], compare_op=ALU.not_equal, fill=1.0, base=0,
                                   pattern=[[-1, P]], channel_multiplier=1).then_inc(sem("consts"), 1)
            pool.affine_select(out=mask_bf[:, :], in_=mask_bf[:, :], compare_op=ALU.is_ge, fill=MASKED, base=0,
                               pattern=[[-1, P]], channel_multiplier=1).then_inc(sem("consts"), 1)
            pool.wait_ge(sem("largest"), 2)
            pool.partition_all_reduce(largest_all[:, :], largest[:, :], P, bass.bass_isa.ReduceOp.max)\
                .then_inc(sem("largest_all"), 1)

        def prepare_tensor(pe):
            pe.wait_ge(sem(LOADED_A), ALL_A)
            for c in range(OC):
                last = pe.matmul(bank[0][:, 0:P], wq_a[:, c, :], wk_a[:, c, :], start=(c == 0), stop=(c == OC - 1))
            last.then_inc(sem("qk_a_ps"), 1)
            pe.wait_ge(sem("consts"), 3)
            for c in range(OC):
                last = pe.transpose(bank[1 + c // 4][:, (c % 4) * P:(c % 4 + 1) * P], wo_a[:, c * P:(c + 1) * P],
                                    ident[:, :])
                if c % 4 == 3:
                    last.then_inc(sem("wo_a_t_ps"), 1)
            pe.wait_ge(sem(LOADED_B), ALL_B)
            for w, at in ((wq_b, 3), (wk_b, 5)):
                for p in range(HP):
                    last = pe.transpose(bank[at + p // 4][:, (p % 4) * P:(p % 4 + 1) * P],
                                        w[:, 2 * p:2 * p + 2, :], ident[:, :])
                    if p % 4 == 3:
                        last.then_inc(sem("wqk_b_t_ps"), 1)
            pe.wait_ge(sem("wo_a_t"), 2)
            for c in range(OC):
                last = pe.matmul(bank[7][:, 0:P], wv_a[:, c, :], wo_a_t[:, c, :], start=(c == 0), stop=(c == OC - 1))
            last.then_inc(sem("vo_a_ps"), 1)
            pe.wait_ge(sem("wq_b_t"), 2)
            pe.wait_ge(sem("wk_b_t"), 2)
            for h in range(H):
                e = slice((h % 2) * E, (h % 2 + 1) * E)
                last = pe.matmul(bank[1 + h % 2 + 2 * (h // 8)][:, (h % 8 // 2) * P:(h % 8 // 2 + 1) * P],
                                 wq_b_t[e, h // 2, :], wk_b_t[e, h // 2, :], start=True, stop=True)
                if h % 8 >= 6:
                    last.then_inc(sem("qk_b_ps"), 1)

        def prepare_scalar(act):
            act.wait_ge(sem("qk_a_ps"), 1)
            act.activation(qk_a[:, :], bank[0][:, 0:P], ACT.Copy, scale=float(O) ** -0.5).then_inc(sem("qk_a"), 1)
            act.wait_ge(sem("qk_a"), 1)
            act.copy(qk_a_hi[:, :], qk_a[:, :]).then_inc(sem("qk_a_hi"), 1)
            for k in range(2):
                act.wait_ge(sem("wqk_b_t_ps"), k + 1)
                act.copy(wq_b_t[:, 4 * k:4 * k + 4, :], bank[3 + k][:, :]).then_inc(sem("wq_b_t"), 1)
            act.wait_ge(sem(LOADED_F), ALL_F)
            act.copy(win_hi[:, :], win2[:, :, :]).then_inc(sem("win_hi"), 1)
            for k in range(4):
                act.wait_ge(sem("qk_b_ps"), k + 1)
                hs = slice(k // 2 * 8 + k % 2, k // 2 * 8 + 8, 2)
                act.activation(qk_b[:, hs, :], bank[1 + k][:, :], ACT.Copy, scale=float(E) ** -0.5)\
                    .then_inc(sem("qk_b"), 1)
                act.wait_ge(sem("qk_b"), k + 1)
                act.copy(qk_b_parts[:, hs, 0, :], qk_b[:, hs, :]).then_inc(sem("qk_b_hi"), 1)
            act.wait_ge(sem("wv_b_scaled"), 1)
            act.copy(wv_b_hi[:, :], wv_b[:, :, :]).then_inc(sem("wv_b_hi"), 1)
            act.wait_ge(sem("wo_b_scaled"), 1)
            act.copy(wo_b_parts[:, :, 0, :], wo_b[:, :, :]).then_inc(sem("wo_b_hi"), 1)

        def prepare_vector(dve):
            dve.wait_ge(sem("qk_a_hi"), 1)
            dve.tensor_tensor(qk_a_lo[:, :], qk_a[:, :], qk_a_hi[:, :].bitcast(F32), ALU.subtract)\
                .then_inc(sem("qk_a_lo"), 1)
            for k in range(2):
                dve.wait_ge(sem("wo_a_t_ps"), k + 1)
                dve.tensor_copy(wo_a_t[:, 4 * k:4 * k + 4, :], bank[1 + k][:, :]).then_inc(sem("wo_a_t"), 1)
            for k in range(2):
                dve.wait_ge(sem("wqk_b_t_ps"), 3 + k)
                dve.tensor_copy(wk_b_t[:, 4 * k:4 * k + 4, :], bank[5 + k][:, :]).then_inc(sem("wk_b_t"), 1)
            dve.tensor_reduce(largest[:, 1:2], wv_b[:, :, :], AX.XY, ALU.max, apply_absolute_value=True)\
                .then_inc(sem("largest"), 1)
            dve.wait_ge(sem("vo_a_ps"), 1)
            dve.tensor_reduce(largest[:, 0:1], bank[7][:, 0:P], AX.X, ALU.max, apply_absolute_value=True)\
                .then_inc(sem("largest"), 1)
            dve.wait_ge(sem("win_hi"), 1)
            dve.tensor_tensor(win_lo[:, :], win2[:, :, :].rearrange("p a m -> p (a m)"), win_hi[:, :].bitcast(F32),
                              ALU.subtract).then_inc(sem("win_lo"), 1)
            dve.wait_ge(sem("largest_all"), 1)
            dve.tensor_scalar_max(scale_up[:, :], largest_all[:, :], TINY).then_inc(sem("scale_up"), 1)
            dve.wait_ge(sem("scale_up"), 1)
            dve.reciprocal(scale_down[:, :], scale_up[:, :]).then_inc(sem("scale_down"), 1)
            dve.wait_ge(sem("scale_down"), 1)
            dve.tensor_scalar(vo_a[:, :], bank[7][:, 0:P], scale_down[:, 0:1], None, ALU.mult)\
                .then_inc(sem("vo_a"), 1)
            dve.tensor_scalar(wv_b[:, :, :], wv_b[:, :, :], scale_down[:, 1:2], None, ALU.mult)\
                .then_inc(sem("wv_b_scaled"), 1)
            dve.tensor_scalar(wo_b[:, :, :], wo_b[:, :, :], scale_up[:, 1:2], None, ALU.mult)\
                .then_inc(sem("wo_b_scaled"), 1)
            for k in range(4):
                dve.wait_ge(sem("qk_b_hi"), k + 1)
                hs = slice(k // 2 * 8 + k % 2, k // 2 * 8 + 8, 2)
                dve.tensor_tensor(qk_b_parts[:, hs, 1, :], qk_b[:, hs, :], qk_b_parts[:, hs, 0, :].bitcast(F32),
                                  ALU.subtract).then_inc(sem("qk_b_lo"), 1)
            dve.wait_ge(sem("wv_b_hi"), 1)
            dve.tensor_tensor(wv_b_lo[:, :], wv_b[:, :, :].rearrange("p h e -> p (h e)"), wv_b_hi[:, :].bitcast(F32),
                              ALU.subtract).then_inc(sem("wv_b_lo"), 1)
            dve.wait_ge(sem("wo_b_hi"), 1)
            dve.tensor_tensor(wo_b_parts[:, :, 1, :], wo_b[:, :, :], wo_b_parts[:, :, 0, :].bitcast(F32),
                              ALU.subtract).then_inc(sem("wo_b_lo"), 1)

        class Norm:

            def __init__(self, name, eps):
                self.name, self.eps = name, eps
                self.stats = sb(f"{name}_stats", [P, QB, 6])
                self.mean_var = sb(f"{name}_mean_var", [P, QB, 2])
                self.neg_mean = sb(f"{name}_neg_mean", [P, QB])
                self.var_eps = sb(f"{name}_var_eps", [P, QB])
                self.rstd = sb(f"{name}_rstd", [P, QB])
                self.y = sb(f"{name}_y", [P, QB, P])
                self.settle = sb(f"{name}_settle", [P, 2])

        def norm_statistics(dve, norm, src, n):
            for i in range(QB):
                last = dve.bn_stats(norm.stats[:, i, :], src(i))
            last.then_inc(sem(f"{norm.name}_st"), 1)
            wait(dve, f"{norm.name}_y", n)
            wait(dve, f"{norm.name}_st", n + 1)
            dve.memset(norm.settle[:, 0:1], 0.0)
            for i in range(QB):
                last = dve.bn_aggr(norm.mean_var[:, i, :], norm.stats[:, i, :])
            last.then_inc(sem(f"{norm.name}_mv"), 1)

        def norm_apply(pool, norm, src, n, free=()):
            name = norm.name
            wait(pool, f"{name}_mv", n + 1)
            pool.tensor_tensor(norm.neg_mean[:, :], norm.mean_var[:, :, 0], minus_one[:, :], ALU.mult)\
                .then_inc(sem(f"{name}_small"), 1)
            pool.tensor_tensor(norm.var_eps[:, :], norm.mean_var[:, :, 1], norm.eps[:, :], ALU.add)\
                .then_inc(sem(f"{name}_small"), 1)
            wait(pool, f"{name}_small", 3 * n + 2)
            pool.tensor_tensor(norm.rstd[:, :], norm.var_eps[:, :], rs_power[:, :], ALU.pow)\
                .then_inc(sem(f"{name}_small"), 1)
            for s, c in free:
                wait(pool, s, c)
            wait(pool, f"{name}_small", 3 * n + 3)
            pool.tensor_tensor(norm.settle[:, 1:2], minus_one[:, 0:1], minus_one[:, 0:1], ALU.mult)
            for i in range(QB):
                last = pool.tensor_scalar(norm.y[:, i, :], src(i), norm.neg_mean[:, i:i + 1], norm.rstd[:, i:i + 1],
                                          ALU.add, ALU.mult)
            last.then_inc(sem(f"{name}_y"), 1)

        ffn_norm = Norm("fn", ln_eps)
        ffn_x_hi = sb("ffn_x_hi", [P, S], F32R)
        ffn_x_lo = sb("ffn_x_lo", [P, S], F32R)
        ffn_s = sb("ffn_s", [P, S])
        ffn_relu = sb("ffn_relu", [P, 2, S])
        ffn_g = sb("ffn_g", [P, S])
        ffn_xb = sb("ffn_xb", [P, QB, P])

        x_attn = sb("x_attn", [P, QB, P])
        x_ffn = sb("x_ffn", [P, QB, P])
        x_done = sb("x_done", [P, QB, P])

        def seq(b):
            return bass.ds(b * QB, QB)

        def ffn_project_pe(pe, bk, n, before=()):
            wait(pe, f"fn_y", n + 1)
            for s, c in before:
                wait(pe, s, c)
            transposes(pe, bk, ffn_norm.y[:, :, :].rearrange("p a d -> p (a d)"), QB)\
                .then_inc(sem("f_xt_ps"), 1)

        def ffn_s_pe(pe, bk, n):
            wait(pe, "f_xt_lo", n + 1)
            split_product(pe, bk[:, :], win_hi[:, :], win_lo[:, :], ffn_x_hi[:, :], ffn_x_lo[:, :])\
                .then_inc(sem("f_s_ps"), 1)

        def ffn_out_pe(pe, bk, n):
            wait(pe, "f_add", J * n + J)
            for i in range(QB):
                last = pe.matmul(bk[:, i * P:(i + 1) * P], ffn_g[:, i * P:(i + 1) * P], wout2[:, :],
                                 start=True, stop=True)
            last.then_inc(sem("f_o_ps"), 1)

        def ffn_xhi_act(act, bk, n):
            wait(act, "f_xt_ps", n + 1)
            wait(act, "f_s_ps", n)
            act.copy(ffn_x_hi[:, :], bk[:, :]).then_inc(sem("f_xt_hi"), 1)

        def ffn_xlo_dve(dve, bk, n):
            wait(dve, "f_xt_hi", n + 1)
            dve.tensor_tensor(ffn_x_lo[:, :], bk[:, :], ffn_x_hi[:, :].bitcast(F32), ALU.subtract)\
                .then_inc(sem("f_xt_lo"), 1)

        def ffn_s_act(act, bk, n):
            wait(act, "f_s_ps", n + 1)
            wait(act, "f_relu", J * n)
            act.activation(ffn_s[:, :], bk[:, :], ACT.Identity, bias=bin_2[:, 0:1]).then_inc(sem("f_s"), 1)

        def ffn_relu_act(act, n, j):
            if j == 0:
                wait(act, "f_s", n + 1)
            wait(act, "f_add", J * n + max(j - 1, 0))
            act.activation(ffn_relu[:, j % 2, :], ffn_s[:, :], ACT.Relu, bias=b1_2[:, j:j + 1],
                           scale=w1_2[:, j:j + 1]).then_inc(sem("f_relu"), 1)

        def ffn_add_dve(dve, n, j):
            wait(dve, "f_relu", J * n + j + 1)
            if j == 0:
                wait(dve, "f_o_ps", n)
                dve.tensor_scalar(ffn_g[:, :], ffn_relu[:, 0, :], w2_2[:, 0:1], b2_2[:, 0:1], ALU.mult, ALU.add)\
                    .then_inc(sem("f_add"), 1)
            else:
                wait(dve, "f_add", J * n + j)
                dve.scalar_tensor_tensor(out=ffn_g[:, :], in0=ffn_relu[:, j % 2, :], scalar=w2_2[:, j:j + 1],
                                         in1=ffn_g[:, :], op0=ALU.mult, op1=ALU.add)\
                    .then_inc(sem("f_add"), 1)

        def ffn_xb_pool(pool, n, x_written):
            wait(pool, "f_x2", n)
            wait(pool, *x_written)
            pool.tensor_tensor(ffn_xb[:, :, :], x_ffn[:, :, :], bout_sb[:, :].unsqueeze(1).broadcast_to([P, QB, P]), ALU.add)\
                .then_inc(sem("f_xb"), 1)

        def ffn_x_dve(dve, bk, n, free=()):
            wait(dve, "f_o_ps", n + 1)
            wait(dve, "f_xb", n + 1)
            wait(dve, "kept", 16 * n)
            for s, c in free:
                wait(dve, s, c)
            dve.tensor_tensor(x_done[:, :, :], bk[:, :].rearrange("p (a d) -> p a d", d=P), ffn_xb[:, :, :], ALU.add)\
                .then_inc(sem("f_x2"), 1)

        at_norm = Norm("at", ln_eps)
        b_norm = Norm("bn", ln_eps)
        at_x = sb("at_x", [P, S])
        at_x_hi = sb("at_x_hi", [P, S], F32R)
        at_x_lo = sb("at_x_lo", [P, S], F32R)
        at_g_hi = sb("at_g_hi", [P, S], F32R)
        at_g_lo = sb("at_g_lo", [P, S], F32R)
        at_v_hi = sb("at_v_hi", [P, QB, P], F16)
        at_v_lo = sb("at_v_lo", [P, QB, P], F16)
        at_neg_max = sb("at_neg_max", [P, QB])
        at_sum = sb("at_sum", [P, QB])
        at_rsum = sb("at_rsum", [P, QB])
        at_scale = sb("at_scale", [P, QB])
        SC, TR, GX, UO, FB = bank[0:3], bank[3:5], bank[5], bank[6], bank[7]

        def flat(norm):
            return norm.y[:, :, :].rearrange("p a d -> p (a d)")

        def front_sync(sp, b, attn, ffn):
            if attn:
                wait(sp, "at_x2", b)
                sp.dma_start(x_attn[:, :, :], x_tiles[:, seq(b), :]).then_inc(sem("x_in"), 16)
            if ffn:
                wait(sp, "f_x2", b)
                sp.dma_start(x_sb[:, seq(b - 1), :], x_done[:, :, :]).then_inc(sem("kept"), 16)

        def front_tensor(pe, b, attn, ffn):
            n, m = b, b - 1
            if attn:
                wait(pe, "at_y", n + 1)
                wait(pe, "at_g_lo", n)
                transposes(pe, GX, flat(at_norm), QB).then_inc(sem("at_xt_ps"), 1)
            if ffn:
                ffn_project_pe(pe, FB, m, before=[("bn_xt_lo", m)])
            if attn:
                wait(pe, "at_x_lo", n + 1)
                split_product(pe, GX[:, :], qk_a_hi[:, :], qk_a_lo[:, :], at_x_hi[:, :], at_x_lo[:, :])\
                    .then_inc(sem("at_g_ps"), 1)
                wait(pe, "at_x2", n)
                for i in range(QB):
                    last = pe.matmul(UO[:, i * P:(i + 1) * P], at_x[:, i * P:(i + 1) * P], vo_a[:, :],
                                     start=True, stop=True)
                last.then_inc(sem("at_v_ps"), 1)
            if ffn:
                ffn_s_pe(pe, FB, m)
            if attn:
                wait(pe, "at_g_lo", n + 1)
                for u in range(NU):
                    wait(pe, "at_p", NU * (n - 1) + u + 1)
                    scores(pe, SC[u], u, at_g_hi, at_g_lo, at_x_hi, at_x_lo, 0).then_inc(sem("at_s"), 1)
                for u in range(NU):
                    wait(pe, "at_p", NU * n + u + 1)
                    wait(pe, "at_pt_lo", NU * n + (u - 1 if u == 2 else 0))
                    transposes(pe, TR[u % 2], prob[u], len(unit_blocks(u))).then_inc(sem("at_pt"), 1)
                wait(pe, "at_v_lo", n + 1)
                for u in range(NU):
                    wait(pe, "at_pt_lo", NU * n + u + 1)
                    weighted_values(pe, lambda i: UO[:, i * P:(i + 1) * P], u,
                                    lambda j: at_v_hi[:, j, :], lambda j: at_v_lo[:, j, :])\
                        .then_inc(sem("at_pv"), 1)
            if ffn:
                ffn_out_pe(pe, FB, m)
                wait(pe, "bn_y", m + 1)
                transposes(pe, FB, flat(b_norm), QB).then_inc(sem("bn_xt_ps"), 1)

        def front_scalar(act, b, attn, ffn):
            n, m = b, b - 1

            def relus(*js):
                if ffn:
                    for j in js:
                        ffn_relu_act(act, m, j)

            if attn:
                wait(act, "at_xt_ps", n + 1)
                wait(act, "at_v_ps", n)
                act.copy(at_x[:, :], GX[:, :]).then_inc(sem("at_x"), 1)
                wait(act, "at_s", NU * n)
                act.copy(at_x_hi[:, :], GX[:, :]).then_inc(sem("at_x_hi"), 1)
            if ffn:
                ffn_xhi_act(act, FB, m)
            if attn:
                wait(act, "at_g_ps", n + 1)
                act.copy(at_g_hi[:, :], GX[:, :]).then_inc(sem("at_g_hi"), 1)
                wait(act, "at_v_ps", n + 1)
                act.copy(at_v_hi[:, :, :], UO[:, :]).then_inc(sem("at_v_hi"), 1)
            if ffn:
                ffn_s_act(act, FB, m)
            relus(0, 1)
            for u in range(NU):
                if attn:
                    wait(act, "at_m", NU * n + u + 1)
                    if u == 0:
                        wait(act, "at_rsum", n)
                    exponentials(act, SC[u], u, at_neg_max, at_sum).then_inc(sem("at_p"), 1)
                relus(2 + u)
            for u in range(NU):
                if attn:
                    wait(act, "at_pt", NU * n + u + 1)
                    wait(act, "at_pv", NU * (n - 1) + u + 1)
                    w = len(unit_blocks(u)) * P
                    act.copy(prob_t_hi[u][:, 0:w], TR[u % 2][:, 0:w]).then_inc(sem("at_pt_hi"), 1)
                relus(5 + u)
            if ffn:
                wait(act, "bn_xt_ps", m + 1)
                act.copy(yt[:, bass.ds(m * S, S)], FB[:, :]).then_inc(sem("bn_yt"), 1)
                act.copy(xt_hi[:, bass.ds(m * S, S)], FB[:, :]).then_inc(sem("bn_xt_hi"), 1)

        def front_vector(dve, b, attn, ffn):
            n, m = b, b - 1

            def adds(*js):
                if ffn:
                    for j in js:
                        ffn_add_dve(dve, m, j)

            if ffn:
                wait(dve, "at_x2", m + 1)
                norm_statistics(dve, ffn_norm, lambda i: x_ffn[:, i, :], m)
            if attn:
                wait(dve, "x_in", 16 * (n + 1))
                norm_statistics(dve, at_norm, lambda i: x_attn[:, i, :], n)
                wait(dve, "at_x_hi", n + 1)
                dve.tensor_tensor(at_x_lo[:, :], GX[:, :], at_x_hi[:, :].bitcast(F32), ALU.subtract)\
                    .then_inc(sem("at_x_lo"), 1)
            if ffn:
                ffn_xlo_dve(dve, FB, m)
            if attn:
                wait(dve, "at_g_hi", n + 1)
                dve.tensor_tensor(at_g_lo[:, :], GX[:, :], at_g_hi[:, :].bitcast(F32), ALU.subtract)\
                    .then_inc(sem("at_g_lo"), 1)
                wait(dve, "at_v_hi", n + 1)
                dve.tensor_tensor(at_v_lo[:, :, :], UO[:, :].rearrange("p (a d) -> p a d", d=P), at_v_hi[:, :, :],
                                  ALU.subtract).then_inc(sem("at_v_lo"), 1)
            adds(0)
            for u in range(NU):
                if attn:
                    wait(dve, "at_s", NU * n + u + 1)
                    row_maxima(dve, SC[u], u, at_neg_max).then_inc(sem("at_m"), 1)
                adds(1 + u)
            for u in range(NU):
                if attn:
                    wait(dve, "at_pt_hi", NU * n + u + 1)
                    w = len(unit_blocks(u)) * P
                    dve.tensor_tensor(prob_t_lo[u][:, 0:w], TR[u % 2][:, 0:w], prob_t_hi[u][:, 0:w], ALU.subtract)\
                        .then_inc(sem("at_pt_lo"), 1)
                adds(4 + u)
            if attn:
                wait(dve, "at_p", NU * n + NU)
                dve.reciprocal(at_rsum[:, :], at_sum[:, :]).then_inc(sem("at_rsum"), 1)
                wait(dve, "at_rsum", n + 1)
                dve.tensor_scalar(at_scale[:, :], at_rsum[:, :], scale_up[:, 0:1], None, ALU.mult)\
                    .then_inc(sem("at_scale"), 1)
            adds(7)
            if ffn:
                ffn_x_dve(dve, FB, m, free=[("bn_y", m)])
            if attn:
                wait(dve, "at_scale", n + 1)
                wait(dve, "at_pv", NU * n + NU)
                wait(dve, "at_y", n + 1)
                wait(dve, "f_xb", n)
                for i in range(QB):
                    last = dve.scalar_tensor_tensor(out=x_ffn[:, i, :], in0=UO[:, i * P:(i + 1) * P],
                                                    scalar=at_scale[:, i:i + 1], in1=x_attn[:, i, :],
                                                    op0=ALU.mult, op1=ALU.add)
                last.then_inc(sem("at_x2"), 1)
            if ffn:
                wait(dve, "f_x2", m + 1)
                norm_statistics(dve, b_norm, lambda i: x_done[:, i, :], m)
                wait(dve, "bn_xt_hi", m + 1)
                dve.tensor_tensor(xt_lo[:, bass.ds(m * S, S)], FB[:, :],
                                  xt_hi[:, bass.ds(m * S, S)].bitcast(F32), ALU.subtract)\
                    .then_inc(sem("bn_xt_lo"), 1)

        def front_gpsimd(pool, b, attn, ffn):
            n, m = b, b - 1
            if ffn:
                norm_apply(pool, ffn_norm, lambda i: x_ffn[:, i, :], m, free=[("f_xt_ps", m)])
            if attn:
                norm_apply(pool, at_norm, lambda i: x_attn[:, i, :], n, free=[("at_xt_ps", n)])
            if ffn:
                ffn_xb_pool(pool, m, ("at_x2", m + 1))
                norm_apply(pool, b_norm, lambda i: x_done[:, i, :], m, free=[("bn_xt_ps", m)])

        NS = 2 * NU
        staging = ExitStack()

        def staged(name, shape):
            return staging.enter_context(nc.sbuf_tensor(name, shape, F32))

        wq_a = staged("wq_a", [P, OC, P])
        wk_a = staged("wk_a", [P, OC, P])
        wv_a = staged("wv_a", [P, OC, P])
        wo_a = staged("wo_a", [P, O])
        wq_b = staged("wq_b", [P, H, E])
        wk_b = staged("wk_b", [P, H, E])
        wv_b = staged("wv_b", [P, H, E])
        wo_b = staged("wo_b", [P, HP, P])
        wo_a_t = staged("wo_a_t", [P, OC, P])
        wq_b_t = staged("wq_b_t", [P, HP, P])
        wk_b_t = staged("wk_b_t", [P, HP, P])
        qk_b = staged("qk_b", [P, H, P])
        staging.close()

        LOADED_A, LOADED_B, LOADED_F = "load_a", "load_b", "load_f"
        a_loads = [(wq_a[:, :, :], a_wq.rearrange("(c p) i -> p c i", p=P)),
                   (wk_a[:, :, :], a_wk.rearrange("(c p) i -> p c i", p=P)),
                   (wo_a[:, :], a_wo),
                   (wv_a[:, :, :], a_wv.rearrange("(c p) i -> p c i", p=P))]
        b_loads = [(wq_b[:, :, :], b_wq.rearrange("h d e -> d h e")),
                   (wk_b[:, :, :], b_wk.rearrange("h d e -> d h e")),
                   (wv_b[:, :, :], b_wv.rearrange("h d e -> d h e")),
                   (wo_b[:, :, :], b_wo.rearrange("(c p) d -> p c d", p=P))]
        f_loads = [(win2[:, 0, :], f_win), (win2[:, 1, :], f_win),
                   (wout2[0:M, :], f_wout), (wout2[M:P, :], f_wout),
                   (w1_2[0:M, :], f_w1[:, 0:J]), (w1_2[M:P, :], f_w1[:, J:INNER]),
                   (b1_2[0:M, :], f_b1[:, 0:J]), (b1_2[M:P, :], f_b1[:, J:INNER]),
                   (w2_2[0:M, :], f_w2[:, 0:J]), (w2_2[M:P, :], f_w2[:, J:INNER]),
                   (bin_2[0:M, :], f_bin.rearrange("(m o) -> m o", o=1)),
                   (bin_2[M:P, :], f_bin.rearrange("(m o) -> m o", o=1)),
                   (b2_2[0:M, :], f_b2.rearrange("(m o) -> m o", o=1)),
                   (gamma_sb[:, :], gamma.rearrange("(o d) -> o d", o=1).broadcast_to([P, P])),
                   (beta_sb[:, :], beta.rearrange("(o d) -> o d", o=1).broadcast_to([P, P])),
                   (bout_sb[:, :], f_bout.rearrange("(o d) -> o d", o=1).broadcast_to([P, P]))]
        x_tiles = x_in.rearrange("b (n p) d -> p (b n) d", p=P)
        out_tiles = out.rearrange("b (n p) d -> p (b n) d", p=P)
        ALL_A, ALL_B, ALL_F = (16 * len(v) for v in (a_loads, b_loads, f_loads))

        qk_now = [sb(f"qk_now{h}", [P, 2, P], F32R) for h in range(2)]
        wo_now = sb("wo_now", [P, 2, P], F32R)
        xv_now = sb("xv_now", [P, 2, P], F32R)
        g_hi = [at_g_hi, sb("g_hi1", [P, S], F32R)]
        g_lo = [at_g_lo, sb("g_lo1", [P, S], F32R)]
        v_hi = sb("v_hi", [P, SLOTS * QB * P], F16)
        v_lo = sb("v_lo", [P, SLOTS * QB * P], F16)
        neg_max = sb("neg_max", [P, 2, QB])
        sums = sb("sums", [P, 2, QB])
        rsum = sb("rsum", [P, 2, QB])
        ctx_sb = sb("ctx_sb", [P, QB, 2, E])
        ctx_t_hi, ctx_t_lo = at_x_hi, at_x_lo
        CT, GB, MB = bank[5], bank[6], bank[7]
        VSLICES = 2 * QB

        def lagged(t, s, lag):
            return (t, s - lag) if s >= lag else (t - 1, s - lag + NS)

        def exists(t):
            return not isinstance(t, int) or t >= 0

        def x_at(t):
            return t // HP * S

        def v_slot_at(t):
            return t % SLOTS * (QB * P)

        def v_dst(buf, k):
            whole = buf[:, :].rearrange("p (s r) -> p s r", r=QB * P)
            slot = k // VSLICES % 2 * HP + k % 2 * (HP // 2)
            return whole[:, bass.ds(slot, HP // 2), bass.ds(k % VSLICES // 2 * P, P)]

        def raw(ap):
            return ap.bitcast(F32)

        def keys_sync(sp, t, h):
            sp.dma_start(raw(qk_now[h][:, :, :]), raw(qk_b_parts[:, bass.ds((2 * t + h) % H, 1), :, :]))\
                .then_inc(sem(f"qk_in{h}"), 16)

        def values_sync(sp, k):
            wait(sp, "v_ps", k)
            at = k // 2 * P
            sp.dma_start(raw(xv_now[:, 0, :]), raw(xt_hi[:, bass.ds(at, P)])).then_inc(sem("xv_in"), 16)
            sp.dma_start(raw(xv_now[:, 1, :]), raw(xt_lo[:, bass.ds(at, P)])).then_inc(sem("xv_in"), 16)

        def values_tensor(pe, k, busy):
            wait(pe, "xv_in", 32 * (k + 1))
            wait(pe, *busy)
            half = bass.ds(k % 2 * 512, 512)
            split_product(pe, MB[:, :], xv_now[:, 0, :], xv_now[:, 1, :], wv_b_hi[:, half], wv_b_lo[:, half])\
                .then_inc(sem("v_ps"), 1)

        def values_scalar(act, k):
            wait(act, "v_ps", k + 1)
            act.copy(v_dst(v_hi, k), MB[:, :].rearrange("p (s c) -> p s c", c=P)).then_inc(sem("v_hi"), 1)

        def values_vector(dve, k):
            wait(dve, "v_hi", k + 1)
            dve.tensor_tensor(v_dst(v_lo, k), MB[:, :].rearrange("p (s c) -> p s c", c=P), v_dst(v_hi, k),
                              ALU.subtract).then_inc(sem("v_lo"), 1)

        def keys_tensor(pe, t, h):
            wait(pe, f"qk_in{h}", 16 * (t + 1))
            if h == 0:
                wait(pe, "g_lo1", t)
            else:
                wait(pe, "g_lo0", t + 1)
            split_product(pe, GB[:, :], qk_now[h][:, 0, :], qk_now[h][:, 1, :],
                          xt_hi[:, bass.ds(x_at(t), S)], xt_lo[:, bass.ds(x_at(t), S)])\
                .then_inc(sem(f"g_ps{h}"), 1)

        def keys_scalar(act, t, h):
            wait(act, f"g_ps{h}", t + 1)
            act.copy(g_hi[h][:, :], GB[:, :]).then_inc(sem(f"g_hi{h}"), 1)

        def keys_vector(dve, t, h):
            wait(dve, f"g_hi{h}", t + 1)
            dve.tensor_tensor(g_lo[h][:, :], GB[:, :], g_hi[h][:, :].bitcast(F32), ALU.subtract)\
                .then_inc(sem(f"g_lo{h}"), 1)

        def heads_tensor(pe, t, fresh=True, vslice=True, next_pair=True):
            for s in range(NS):
                u, h = s % NU, s // NU
                t2, s2 = lagged(t, s, 2)
                t3, s3 = lagged(t, s, 3)
                t4, s4 = lagged(t, s, 4)
                if fresh:
                    if u == 0:
                        wait(pe, f"g_lo{h}", t + 1)
                    if exists(t3):
                        wait(pe, f"p{s3}", t3 + 1)
                    scores(pe, SC[u], u, g_hi[h], g_lo[h], xt_hi, xt_lo, x_at(t)).then_inc(sem(f"s{s}"), 1)
                if exists(t2) and (fresh or s < 2):
                    wait(pe, f"p{s2}", t2 + 1)
                    if exists(t4):
                        wait(pe, f"pt_lo{s4}", t4 + 1)
                    transposes(pe, TR[s2 % 2], prob[s2 % NU], len(unit_blocks(s2 % NU)))\
                        .then_inc(sem(f"pt{s2}"), 1)
                if exists(t3) and (fresh or s < 3):
                    if s3 == 0:
                        wait(pe, "ctx", t3)
                        wait(pe, "v_lo", t3 // HP * VSLICES + VSLICES)
                    wait(pe, f"pt_lo{s3}", t3 + 1)
                    h3 = s3 // NU
                    at = v_slot_at(t3)
                    weighted_values(pe, lambda i: CT[:, i * P + h3 * E:i * P + (h3 + 1) * E], s3 % NU,
                                    lambda j: v_hi[:, bass.ds(at + (j * P + h3 * E), E)],
                                    lambda j: v_lo[:, bass.ds(at + (j * P + h3 * E), E)])\
                        .then_inc(sem(f"pv{s3}"), 1)
                if s == 0 and fresh:
                    keys_tensor(pe, t, 1)
                if s == 1 and vslice:
                    values_tensor(pe, t + VSLICES, ("y_acc", t - 1))
                if s == 2 and next_pair:
                    keys_tensor(pe, t + 1, 0)
                if s == 3 and exists(t - 1):
                    wait(pe, "ctx", t)
                    if vslice:
                        wait(pe, "v_lo", t + VSLICES + 1)
                    else:
                        wait(pe, "y_acc", t - 1)
                    transposes(pe, MB, ctx_sb[:, :, :, :].rearrange("p a h e -> p (a h e)"), QB)\
                        .then_inc(sem("ctx_t_ps"), 1)
                if s == 5 and exists(t - 1):
                    wait(pe, "wo_in", 16 * t)
                    wait(pe, "ctx_t_lo", t)
                    split_product(pe, MB[:, :], wo_now[:, 0, :], wo_now[:, 1, :], ctx_t_hi[:, :], ctx_t_lo[:, :])\
                        .then_inc(sem("y_ps"), 1)

        def heads_scalar(act, t, fresh=True, vslice=True, next_pair=True):
            for s in range(NS):
                u, h = s % NU, s // NU
                t2, s2 = lagged(t, s, 2)
                t3, s3 = lagged(t, s, 3)
                t5, s5 = lagged(t, s, 5)
                if s == 1 and fresh:
                    keys_scalar(act, t, 1)
                if s == 2 and vslice:
                    wait(act, "pv5", t - 1)
                    values_scalar(act, t + VSLICES)
                if s == 3 and next_pair:
                    keys_scalar(act, t + 1, 0)
                if s == 4 and exists(t - 1):
                    wait(act, "ctx_t_ps", t)
                    wait(act, "y_ps", t - 1)
                    act.copy(ctx_t_hi[:, :], MB[:, :]).then_inc(sem("ctx_t_hi"), 1)
                if exists(t2) and (fresh or s < 2):
                    wait(act, f"pt{s2}", t2 + 1)
                    if exists(t5):
                        wait(act, f"pv{s5}", t5 + 1)
                    w = len(unit_blocks(s2 % NU)) * P
                    act.copy(prob_t_hi[s2 % NU][:, 0:w], TR[s2 % 2][:, 0:w]).then_inc(sem(f"pt_hi{s2}"), 1)
                if fresh:
                    wait(act, f"m{s}", t + 1)
                    if exists(t3):
                        wait(act, f"pt{s3}", t3 + 1)
                    if u == 0:
                        wait(act, f"rsum{h}", t)
                    exponentials(act, SC[u], u, neg_max[:, h, :], sums[:, h, :]).then_inc(sem(f"p{s}"), 1)

        def heads_vector(dve, t, fresh=True, vslice=True, next_pair=True):
            for s in range(NS):
                u, h = s % NU, s // NU
                t2, s2 = lagged(t, s, 2)
                if s == 3 and exists(t - 1):
                    wait(dve, "pv5", t)
                    wait(dve, "rsum1", t)
                    wait(dve, "ctx_t_ps", t - 1)
                    dve.tensor_tensor(ctx_sb[:, :, :, :], CT[:, :].rearrange("p (a h e) -> p a h e", h=2, e=E),
                                      rsum[:, :, :].rearrange("p h a -> p a h").unsqueeze(3)
                                      .broadcast_to([P, QB, 2, E]), ALU.mult).then_inc(sem("ctx"), 1)
                if fresh:
                    wait(dve, f"s{s}", t + 1)
                    row_maxima(dve, SC[u], u, neg_max[:, h, :]).then_inc(sem(f"m{s}"), 1)
                if exists(t2) and (fresh or s < 2):
                    wait(dve, f"pt_hi{s2}", t2 + 1)
                    w = len(unit_blocks(s2 % NU)) * P
                    dve.tensor_tensor(prob_t_lo[s2 % NU][:, 0:w], TR[s2 % 2][:, 0:w], prob_t_hi[s2 % NU][:, 0:w],
                                      ALU.subtract).then_inc(sem(f"pt_lo{s2}"), 1)
                if s == 0 and exists(t - 2):
                    output_vector(dve, t - 2)
                if s == 0 and exists(t - 1):
                    wait(dve, "p5", t)
                    dve.reciprocal(rsum[:, 1, :], sums[:, 1, :]).then_inc(sem("rsum1"), 1)
                if s == 1 and fresh:
                    keys_vector(dve, t, 1)
                if s == 2 and vslice:
                    values_vector(dve, t + VSLICES)
                if s == 3 and next_pair:
                    keys_vector(dve, t + 1, 0)
                if s == 3 and fresh:
                    wait(dve, "p2", t + 1)
                    wait(dve, "ctx", t)
                    dve.reciprocal(rsum[:, 0, :], sums[:, 0, :]).then_inc(sem("rsum0"), 1)
                if s == 4 and exists(t - 1):
                    wait(dve, "ctx_t_hi", t)
                    dve.tensor_tensor(ctx_t_lo[:, :], MB[:, :], ctx_t_hi[:, :].bitcast(F32), ALU.subtract)\
                        .then_inc(sem("ctx_t_lo"), 1)

        def output_vector(dve, t):
            wait(dve, "y_ps", t + 1)
            at = bass.ds(x_at(t), S)
            dve.tensor_tensor(yt[:, at], MB[:, :], yt[:, at], ALU.add).then_inc(sem("y_acc"), 1)

        y_norm = Norm("yn", ln_b_eps)
        y_now, y_tok, y_gb = at_x, at_norm.y, b_norm.y
        x_beta = sb("x_beta", [P, QB, P])
        YB, FK = bank[0], bank[1]

        def back_sync(sp, b, first, second):
            if first:
                wait(sp, "x_beta", b)
                wait(sp, "kept", 16 * B)
                sp.dma_start(x_attn[:, :, :], x_sb[:, seq(b), :]).then_inc(sem("x_in"), 16)
            if second:
                wait(sp, "f_x2", B + b)
                sp.dma_start(out_tiles[:, seq(b - 1), :], x_done[:, :, :]).then_inc(sem("kept"), 16)

        def back_tensor(pe, b, first, second):
            n, m = b, b - 1
            r = B + m
            if first:
                wait(pe, "y_now", n + 1)
                wait(pe, "y_tok", n)
                transposes(pe, YB, y_now, QB).then_inc(sem("y_tok_ps"), 1)
            if second:
                ffn_project_pe(pe, FK, r, before=[("f_x2", r)])
                ffn_s_pe(pe, FK, r)
                ffn_out_pe(pe, FK, r)

        def back_scalar(act, b, first, second):
            n, m = b, b - 1
            r = B + m
            if first:
                wait(act, "y_tok_ps", n)
                act.copy(y_now[:, :], yt[:, bass.ds(n * S, S)]).then_inc(sem("y_now"), 1)
                wait(act, "y_tok_ps", n + 1)
                wait(act, "yn_y", n)
                act.copy(y_tok[:, :, :], YB[:, :]).then_inc(sem("y_tok"), 1)
            if second:
                ffn_xhi_act(act, FK, r)
                ffn_s_act(act, FK, r)
                for j in range(J):
                    ffn_relu_act(act, r, j)

        def back_vector(dve, b, first, second):
            n, m = b, b - 1
            r = B + m
            if second:
                wait(dve, "y_x2", m + 1)
                norm_statistics(dve, ffn_norm, lambda i: x_ffn[:, i, :], r)
            if first:
                wait(dve, "y_tok", n + 1)
                norm_statistics(dve, y_norm, lambda i: y_tok[:, i, :], n)
            if second:
                ffn_xlo_dve(dve, FK, r)
                for j in range(J // 2):
                    ffn_add_dve(dve, r, j)
            if first:
                wait(dve, "yn_y", n + 1)
                dve.tensor_tensor(y_gb[:, :, :], y_norm.y[:, :, :],
                                  gamma_sb[:, :].unsqueeze(1).broadcast_to([P, QB, P]), ALU.mult)\
                    .then_inc(sem("y_gb"), 1)
                wait(dve, "y_gb", n + 1)
                wait(dve, "x_beta", n + 1)
                wait(dve, "f_xb", B + n)
                dve.tensor_tensor(x_ffn[:, :, :], y_gb[:, :, :], x_beta[:, :, :], ALU.add).then_inc(sem("y_x2"), 1)
            if second:
                for j in range(J // 2, J):
                    ffn_add_dve(dve, r, j)
                ffn_x_dve(dve, FK, r)

        def back_gpsimd(pool, b, first, second):
            n, m = b, b - 1
            r = B + m
            if second:
                norm_apply(pool, ffn_norm, lambda i: x_ffn[:, i, :], r, free=[("f_xt_ps", r)])
            if first:
                wait(pool, "y_x2", n)
                wait(pool, "x_in", 16 * (B + n + 1))
                pool.tensor_tensor(x_beta[:, :, :], x_attn[:, :, :], beta_sb[:, :].unsqueeze(1).broadcast_to([P, QB, P]),
                                   ALU.add).then_inc(sem("x_beta"), 1)
                norm_apply(pool, y_norm, lambda i: y_tok[:, i, :], n, free=[("y_gb", n)])
            if second:
                ffn_xb_pool(pool, r, ("y_x2", m + 1))

        block = ctx.enter_context(nc.Block())

        def over_sequences(eng, body):
            body(eng, 0, True, False)
            with eng.Fori(1, B) as b:
                body(eng, b, True, True)
            body(eng, B, False, True)

        def over_pairs(eng, body):
            body(eng, 0)
            body(eng, 1)
            with eng.Fori(2, PAIRS - HP) as t:
                body(eng, t)
            with eng.Fori(PAIRS - HP, PAIRS - 1) as t:
                body(eng, t, vslice=False)
            body(eng, PAIRS - 1, vslice=False, next_pair=False)

        @block.sync
        def _(sp):
            prepare_loads_sync(sp)
            sp.wait_ge(sem("qk_b_lo"), 4)
            for h in range(2):
                keys_sync(sp, 0, h)
            sp.wait_ge(sem("wo_b_lo"), 1)
            over_sequences(sp, front_sync)
            wait(sp, "bn_xt_lo", B)
            with sp.Fori(0, VSLICES) as k:
                values_sync(sp, k)

            def body(sp, t, vslice=True, next_pair=True):
                if vslice:
                    values_sync(sp, t + VSLICES)
                if next_pair:
                    for h in range(2):
                        wait(sp, f"g_ps{h}", t + 1)
                        keys_sync(sp, t + 1, h)
                wait(sp, "y_ps", t)
                sp.dma_start(raw(wo_now[:, :, :]), raw(wo_b_parts[:, bass.ds(t % HP, 1), :, :]))\
                    .then_inc(sem("wo_in"), 16)

            over_pairs(sp, body)
            over_sequences(sp, back_sync)
            sp.wait_ge(sem("kept"), 16 * 2 * B)

        @block.gpsimd
        def _(pool):
            prepare_gpsimd(pool)
            pool.wait_ge(sem(LOADED_F), ALL_F)
            over_sequences(pool, front_gpsimd)
            over_sequences(pool, back_gpsimd)

        @block.tensor
        def _(pe):
            prepare_tensor(pe)
            pe.wait_ge(sem("qk_a_lo"), 1)
            pe.wait_ge(sem("vo_a"), 1)
            pe.wait_ge(sem("win_lo"), 1)
            pe.wait_ge(sem("qk_b_hi"), 4)
            over_sequences(pe, front_tensor)
            pe.wait_ge(sem("wv_b_lo"), 1)
            pe.wait_ge(sem("bn_xt_lo"), B)
            with pe.Fori(0, VSLICES) as k:
                values_tensor(pe, k, ("v_lo", k))
            keys_tensor(pe, 0, 0)
            over_pairs(pe, heads_tensor)
            heads_tensor(pe, PAIRS, fresh=False, vslice=False, next_pair=False)
            over_sequences(pe, back_tensor)

        @block.scalar
        def _(act):
            prepare_loads_scalar(act)
            prepare_scalar(act)
            over_sequences(act, front_scalar)
            with act.Fori(0, VSLICES) as k:
                values_scalar(act, k)
            keys_scalar(act, 0, 0)
            over_pairs(act, heads_scalar)
            heads_scalar(act, PAIRS, fresh=False, vslice=False, next_pair=False)
            act.wait_ge(sem("y_acc"), PAIRS)
            over_sequences(act, back_scalar)

        @block.vector
        def _(dve):
            prepare_vector(dve)
            over_sequences(dve, front_vector)
            with dve.Fori(0, VSLICES) as k:
                values_vector(dve, k)
            keys_vector(dve, 0, 0)
            over_pairs(dve, heads_vector)
            heads_vector(dve, PAIRS, fresh=False, vslice=False, next_pair=False)
            output_vector(dve, PAIRS - 1)
            over_sequences(dve, back_vector)


_INS = ['L0_attn_a_in_features', 'L0_attn_a_w_q', 'L0_attn_a_w_k', 'L0_attn_a_w_v', 'L0_attn_a_w_o',
        'L0_attn_b_Wq', 'L0_attn_b_Wk', 'L0_attn_b_Wv', 'L0_attn_b_Wo', 'L0_attn_b_gamma', 'L0_attn_b_beta',
        'L0_ffn_Win', 'L0_ffn_bin_', 'L0_ffn_W1', 'L0_ffn_b1', 'L0_ffn_W2', 'L0_ffn_b2', 'L0_ffn_Wout',
        'L0_ffn_bout']


def kernel(**inputs):
    import numpy as np
    import concourse.bacc as bacc
    from concourse.bass_utils import run_bass_kernel_spmd

    nc = bacc.Bacc("TRN2", target_bir_lowering=False, num_devices=1)
    arrays, args = {}, []
    for name in _INS:
        a = np.ascontiguousarray(inputs[name])
        arrays[f"in_{name}"] = a
        args.append(nc.dram_tensor(f"in_{name}", a.shape, mybir.dt.from_np(a.dtype), kind="ExternalInput").ap())
    shape = inputs[_INS[0]].shape
    args.append(nc.dram_tensor("out_x", shape, F32, kind="ExternalOutput").ap())
    hybrid_kernel(nc, *args)
    r = run_bass_kernel_spmd(nc, [arrays], core_ids=[0])
    return r.results[0]["out_x"]
```

```python
from contextlib import ExitStack

import concourse.bass as bass
from concourse import mybir

F32 = mybir.dt.float32
F32R = mybir.dt.float32r
F16 = mybir.dt.float16
BF16 = mybir.dt.bfloat16
ALU = mybir.AluOpType
ACT = mybir.ActivationFunctionType
AX = mybir.AxisListType

P = 128
MASKED = -3.0e38
LN_EPS = 1e-5
LN_B_EPS = 1e-3
TINY = 1e-30

UNIT_ROWS = [(0, 1), (2,), (3,)]
NU = len(UNIT_ROWS)
SCORE_AT = {0: 0, 1: 256, 2: 0, 3: 0}
SCORE_N = {0: 256, 1: 256, 2: 384, 3: 512}


def unit_blocks(u):
    return [(i, j) for i in UNIT_ROWS[u] for j in range(i + 1)]


def hybrid_kernel(nc, x_in, a_wq, a_wk, a_wv, a_wo, b_wq, b_wk, b_wv, b_wo, gamma, beta,
                  f_win, f_bin, f_w1, f_b1, f_w2, f_b2, f_wout, f_bout, out):
    B, S, D = x_in.shape
    H, _, E = b_wq.shape
    O = a_wq.shape[0]
    M, INNER = f_w1.shape
    QB = S // P
    NT = B * QB
    OC = O // P
    HP = H // 2
    PAIRS = B * HP
    J = INNER // 2
    SLOTS = 2 * HP
    assert D == P and S == 4 * P and 2 * E == P and 2 * M == P and H * E == O

    with ExitStack() as ctx:
        def sb(name, shape, dt=F32):
            return ctx.enter_context(nc.sbuf_tensor(name, shape, dt))

        sems = {}

        def sem(name):
            if name not in sems:
                sems[name] = ctx.enter_context(nc.semaphore(name))
            return sems[name]

        def wait(eng, name, count):
            if isinstance(count, int) and count <= 0:
                return
            eng.wait_ge(sem(name), count)

        bank = [ctx.enter_context(nc.psum_tensor(f"bank{i}", [P, 512], F32)) for i in range(8)]

        ident = sb("ident", [P, P])
        ident_bf = sb("ident_bf", [P, P], BF16)
        mask_bf = sb("mask_bf", [P, P], BF16)
        rs_power = sb("rs_power", [P, QB])
        minus_one = sb("minus_one", [P, QB])
        ln_eps = sb("ln_eps", [P, QB])
        ln_b_eps = sb("ln_b_eps", [P, QB])
        gamma_sb = sb("gamma_sb", [P, P])
        beta_sb = sb("beta_sb", [P, P])
        bout_sb = sb("bout_sb", [P, P])
        win2 = sb("win2", [P, 2, M])
        wout2 = sb("wout2", [P, P])
        w1_2 = sb("w1_2", [P, J])
        b1_2 = sb("b1_2", [P, J])
        w2_2 = sb("w2_2", [P, J])
        b2_2 = sb("b2_2", [P, 1])
        bin_2 = sb("bin_2", [P, 1])

        qk_a = sb("qk_a", [P, P])
        qk_a_hi = sb("qk_a_hi", [P, P], F32R)
        qk_a_lo = sb("qk_a_lo", [P, P], F32R)
        vo_a = sb("vo_a", [P, P])
        qk_b_parts = sb("qk_b_parts", [P, H, 2, P], F32R)
        wv_b_hi = sb("wv_b_hi", [P, O], F32R)
        wv_b_lo = sb("wv_b_lo", [P, O], F32R)
        wo_b_parts = sb("wo_b_parts", [P, HP, 2, P], F32R)
        win_hi = sb("win_hi", [P, P], F32R)
        win_lo = sb("win_lo", [P, P], F32R)
        largest = sb("largest", [P, 2])
        largest_all = sb("largest_all", [P, 2])
        scale_up = sb("scale_up", [P, 2])
        scale_down = sb("scale_down", [P, 2])

        x_sb = sb("x_sb", [P, NT, P])
        yt = sb("yt", [P, B * S])
        xt_hi = sb("xt_hi", [P, B * S], F32R)
        xt_lo = sb("xt_lo", [P, B * S], F32R)

        prob = [sb(f"prob{u}", [P, 512]) for u in range(NU)]
        prob_t_hi = [sb(f"prob_t_hi{u}", [P, 512], F16) for u in range(NU)]
        prob_t_lo = [sb(f"prob_t_lo{u}", [P, 512], F16) for u in range(NU)]

        def split_product(pe, dst, lhs_hi, lhs_lo, rhs_hi, rhs_lo, start=True, stop=True):
            pe.matmul(dst, lhs_hi, rhs_hi, start=start, stop=False)
            pe.matmul(dst, lhs_hi, rhs_lo, start=False, stop=False)
            return pe.matmul(dst, lhs_lo, rhs_hi, start=False, stop=stop)

        def scores(pe, dst, u, g_hi, g_lo, x_hi, x_lo, at):
            for i in UNIT_ROWS[u]:
                c, n = SCORE_AT[i], SCORE_N[i]
                split_product(pe, dst[:, c:c + n], g_hi[:, i * P:(i + 1) * P], g_lo[:, i * P:(i + 1) * P],
                              x_hi[:, bass.ds(at, n)], x_lo[:, bass.ds(at, n)], stop=False)
                last = pe.matmul(dst[:, c + i * P:c + (i + 1) * P], ident_bf[:, :], mask_bf[:, :],
                                 start=False, stop=True)
            return last

        def row_maxima(dve, src, u, neg_max):
            for i in UNIT_ROWS[u]:
                c = SCORE_AT[i]
                last = dve.tensor_reduce(neg_max[:, i:i + 1], src[:, c:c + (i + 1) * P], AX.X, ALU.max,
                                         negate=True)
            return last

        def exponentials(act, src, u, neg_max, sums):
            at = 0
            for i in UNIT_ROWS[u]:
                c, n = SCORE_AT[i], (i + 1) * P
                last = act.activation(prob[u][:, at:at + n], src[:, c:c + n], ACT.Exp,
                                      bias=neg_max[:, i:i + 1], accum_out=sums[:, i:i + 1])
                at += n
            return last

        def transposes(pe, dst, src, n):
            for k in range(n):
                last = pe.transpose(dst[:, k * P:(k + 1) * P], src[:, k * P:(k + 1) * P], ident[:, :])
            return last

        def weighted_values(pe, dst, u, v_hi, v_lo):
            k = 0
            for i, j in unit_blocks(u):
                blk = slice(k * P, (k + 1) * P)
                pe.matmul(dst(i), prob_t_hi[u][:, blk], v_hi(j), start=(j == 0), stop=False)
                pe.matmul(dst(i), prob_t_hi[u][:, blk], v_lo(j), start=False, stop=False)
                last = pe.matmul(dst(i), prob_t_lo[u][:, blk], v_hi(j), start=False, stop=(j == i))
                k += 1
            return last


        def prepare_loads_scalar(act):
            for k, (dst, src) in enumerate(a_loads):
                act.dma_start(dst, src).then_inc(sem(LOADED_QK_A if k < 2 else LOADED_A), 16)

        def prepare_loads_sync(sp):
            for dst, src in b_loads:
                sp.dma_start(dst, src).then_inc(sem(LOADED_B), 16)
            sp.wait_ge(sem("b2_zeroed"), 1)
            for dst, src in f_loads:
                sp.dma_start(dst, src).then_inc(sem(LOADED_F), 16)

        def prepare_gpsimd(pool):
            pool.memset(ident[:, :], 0.0).then_inc(sem("const_0"), 1)
            pool.memset(ident_bf[:, :], 0.0).then_inc(sem("const_0"), 1)
            pool.memset(mask_bf[:, :], 0.0).then_inc(sem("const_0"), 1)
            for m, value in ((rs_power, -0.5), (minus_one, -1.0), (ln_eps, LN_EPS), (ln_b_eps, LN_B_EPS)):
                pool.memset(m[:, :], value).then_inc(sem("const_0"), 1)
            pool.memset(b2_2[:, :], 0.0).then_inc(sem("b2_zeroed"), 1)
            pool.wait_ge(sem("const_0"), 7)
            for m in (ident, ident_bf):
                pool.affine_select(out=m[:, :], in_=m[:, :], compare_op=ALU.not_equal, fill=1.0, base=0,
                                   pattern=[[-1, P]], channel_multiplier=1).then_inc(sem("consts"), 1)
            pool.affine_select(out=mask_bf[:, :], in_=mask_bf[:, :], compare_op=ALU.is_ge, fill=MASKED, base=0,
                               pattern=[[-1, P]], channel_multiplier=1).then_inc(sem("consts"), 1)
            front_gpsimd(pool, -2)
            pool.wait_ge(sem("largest"), 2)
            pool.partition_all_reduce(largest_all[:, :], largest[:, :], P, bass.bass_isa.ReduceOp.max)\
                .then_inc(sem("largest_all"), 1)

        def prepare_tensor(pe):
            pe.wait_ge(sem(LOADED_QK_A), 2 * 16)
            for c in range(OC):
                last = pe.matmul(bank[0][:, 0:P], wq_a[:, c, :], wk_a[:, c, :], start=(c == 0), stop=(c == OC - 1))
            last.then_inc(sem("qk_a_ps"), 1)
            pe.wait_ge(sem("consts"), 3)
            pe.wait_ge(sem(LOADED_A), 2 * 16)
            for c in range(OC):
                last = pe.transpose(bank[1 + c // 4][:, (c % 4) * P:(c % 4 + 1) * P], wo_a[:, c * P:(c + 1) * P],
                                    ident[:, :])
                if c % 4 == 3:
                    last.then_inc(sem("wo_a_t_ps"), 1)
            pe.wait_ge(sem(LOADED_B), ALL_B)
            for w, at in ((wq_b, 3), (wk_b, 5)):
                for p in range(HP):
                    last = pe.transpose(bank[at + p // 4][:, (p % 4) * P:(p % 4 + 1) * P],
                                        w[:, 2 * p:2 * p + 2, :], ident[:, :])
                    if p % 4 == 3:
                        last.then_inc(sem("wqk_b_t_ps"), 1)
            pe.wait_ge(sem("wo_a_t"), 2)
            for c in range(OC):
                last = pe.matmul(bank[7][:, 0:P], wv_a[:, c, :], wo_a_t[:, c, :], start=(c == 0), stop=(c == OC - 1))
            last.then_inc(sem("vo_a_ps"), 1)
            pe.wait_ge(sem("wq_b_t"), 2)
            pe.wait_ge(sem("wk_b_t"), 2)
            for h in range(H):
                e = slice((h % 2) * E, (h % 2 + 1) * E)
                last = pe.matmul(bank[1 + h % 2 + 2 * (h // 8)][:, (h % 8 // 2) * P:(h % 8 // 2 + 1) * P],
                                 wq_b_t[e, h // 2, :], wk_b_t[e, h // 2, :], start=True, stop=True)
                if h % 8 >= 6:
                    last.then_inc(sem("qk_b_ps"), 1)

        def prepare_scalar(act):
            act.wait_ge(sem("qk_a_ps"), 1)
            act.activation(qk_a[:, :], bank[0][:, 0:P], ACT.Copy, scale=float(O) ** -0.5).then_inc(sem("qk_a"), 1)
            act.wait_ge(sem("qk_a"), 1)
            act.copy(qk_a_hi[:, :], qk_a[:, :]).then_inc(sem("qk_a_hi"), 1)
            for k in range(2):
                act.wait_ge(sem("wqk_b_t_ps"), k + 1)
                act.copy(wq_b_t[:, 4 * k:4 * k + 4, :], bank[3 + k][:, :]).then_inc(sem("wq_b_t"), 1)
            act.wait_ge(sem(LOADED_F), ALL_F)
            act.copy(win_hi[:, :], win2[:, :, :]).then_inc(sem("win_hi"), 1)
            for k in range(4):
                act.wait_ge(sem("qk_b_ps"), k + 1)
                hs = slice(k // 2 * 8 + k % 2, k // 2 * 8 + 8, 2)
                act.activation(qk_b[:, hs, :], bank[1 + k][:, :], ACT.Copy, scale=float(E) ** -0.5)\
                    .then_inc(sem("qk_b"), 1)
                act.wait_ge(sem("qk_b"), k + 1)
                act.copy(qk_b_parts[:, hs, 0, :], qk_b[:, hs, :]).then_inc(sem("qk_b_hi"), 1)
            act.wait_ge(sem("wv_b_scaled"), 1)
            act.copy(wv_b_hi[:, :], wv_b[:, :, :]).then_inc(sem("wv_b_hi"), 1)
            act.wait_ge(sem("wo_b_scaled"), 1)
            act.copy(wo_b_parts[:, :, 0, :], wo_b[:, :, :]).then_inc(sem("wo_b_hi"), 1)

        def prepare_vector(dve):
            dve.wait_ge(sem("qk_a_hi"), 1)
            dve.tensor_tensor(qk_a_lo[:, :], qk_a[:, :], qk_a_hi[:, :].bitcast(F32), ALU.subtract)\
                .then_inc(sem("qk_a_lo"), 1)
            for k in range(2):
                dve.wait_ge(sem("wo_a_t_ps"), k + 1)
                dve.tensor_copy(wo_a_t[:, 4 * k:4 * k + 4, :], bank[1 + k][:, :]).then_inc(sem("wo_a_t"), 1)
            for k in range(2):
                dve.wait_ge(sem("wqk_b_t_ps"), 3 + k)
                dve.tensor_copy(wk_b_t[:, 4 * k:4 * k + 4, :], bank[5 + k][:, :]).then_inc(sem("wk_b_t"), 1)
            dve.tensor_reduce(largest[:, 1:2], wv_b[:, :, :], AX.XY, ALU.max, apply_absolute_value=True)\
                .then_inc(sem("largest"), 1)
            dve.wait_ge(sem("vo_a_ps"), 1)
            dve.tensor_reduce(largest[:, 0:1], bank[7][:, 0:P], AX.X, ALU.max, apply_absolute_value=True)\
                .then_inc(sem("largest"), 1)
            dve.wait_ge(sem("win_hi"), 1)
            dve.tensor_tensor(win_lo[:, :], win2[:, :, :].rearrange("p a m -> p (a m)"), win_hi[:, :].bitcast(F32),
                              ALU.subtract).then_inc(sem("win_lo"), 1)
            dve.wait_ge(sem("largest_all"), 1)
            dve.tensor_scalar_max(scale_up[:, :], largest_all[:, :], TINY).then_inc(sem("scale_up"), 1)
            dve.wait_ge(sem("scale_up"), 1)
            dve.reciprocal(scale_down[:, :], scale_up[:, :]).then_inc(sem("scale_down"), 1)
            dve.wait_ge(sem("scale_down"), 1)
            dve.tensor_scalar(vo_a[:, :], bank[7][:, 0:P], scale_down[:, 0:1], None, ALU.mult)\
                .then_inc(sem("vo_a"), 1)
            dve.tensor_scalar(wv_b[:, :, :], wv_b[:, :, :], scale_down[:, 1:2], None, ALU.mult)\
                .then_inc(sem("wv_b_scaled"), 1)
            dve.tensor_scalar(wo_b[:, :, :], wo_b[:, :, :], scale_up[:, 1:2], None, ALU.mult)\
                .then_inc(sem("wo_b_scaled"), 1)
            for k in range(4):
                dve.wait_ge(sem("qk_b_hi"), k + 1)
                hs = slice(k // 2 * 8 + k % 2, k // 2 * 8 + 8, 2)
                dve.tensor_tensor(qk_b_parts[:, hs, 1, :], qk_b[:, hs, :], qk_b_parts[:, hs, 0, :].bitcast(F32),
                                  ALU.subtract).then_inc(sem("qk_b_lo"), 1)
            dve.wait_ge(sem("wv_b_hi"), 1)
            dve.tensor_tensor(wv_b_lo[:, :], wv_b[:, :, :].rearrange("p h e -> p (h e)"), wv_b_hi[:, :].bitcast(F32),
                              ALU.subtract).then_inc(sem("wv_b_lo"), 1)
            dve.wait_ge(sem("wo_b_hi"), 1)
            dve.tensor_tensor(wo_b_parts[:, :, 1, :], wo_b[:, :, :], wo_b_parts[:, :, 0, :].bitcast(F32),
                              ALU.subtract).then_inc(sem("wo_b_lo"), 1)

        class Norm:

            def __init__(self, name, eps):
                self.name, self.eps = name, eps
                self.stats = sb(f"{name}_stats", [P, QB, 6])
                self.mean_var = sb(f"{name}_mean_var", [P, QB, 2])
                self.neg_mean = sb(f"{name}_neg_mean", [P, QB])
                self.var_eps = sb(f"{name}_var_eps", [P, QB])
                self.rstd = sb(f"{name}_rstd", [P, QB])
                self.y = sb(f"{name}_y", [P, QB, P])
                self.settle = sb(f"{name}_settle", [P, 2])

            def tokens(self):
                return self.y[:, :, :].rearrange("p a d -> p (a d)")

        def norm_statistics(dve, norm, src, n):
            for i in range(QB):
                last = dve.bn_stats(norm.stats[:, i, :], src(i))
            last.then_inc(sem(f"{norm.name}_st"), 1)
            wait(dve, f"{norm.name}_y", n)
            wait(dve, f"{norm.name}_st", n + 1)
            dve.memset(norm.settle[:, 0:1], 0.0)
            for i in range(QB):
                last = dve.bn_aggr(norm.mean_var[:, i, :], norm.stats[:, i, :])
            last.then_inc(sem(f"{norm.name}_mv"), 1)

        def norm_apply(pool, norm, src, n, free=()):
            name = norm.name
            wait(pool, f"{name}_mv", n + 1)
            pool.tensor_tensor(norm.neg_mean[:, :], norm.mean_var[:, :, 0], minus_one[:, :], ALU.mult)\
                .then_inc(sem(f"{name}_small"), 1)
            pool.tensor_tensor(norm.var_eps[:, :], norm.mean_var[:, :, 1], norm.eps[:, :], ALU.add)\
                .then_inc(sem(f"{name}_small"), 1)
            wait(pool, f"{name}_small", 3 * n + 2)
            pool.tensor_tensor(norm.rstd[:, :], norm.var_eps[:, :], rs_power[:, :], ALU.pow)\
                .then_inc(sem(f"{name}_small"), 1)
            for s, c in free:
                wait(pool, s, c)
            wait(pool, f"{name}_small", 3 * n + 3)
            pool.tensor_tensor(norm.settle[:, 1:2], minus_one[:, 0:1], minus_one[:, 0:1], ALU.mult)
            for i in range(QB):
                last = pool.tensor_scalar(norm.y[:, i, :], src(i), norm.neg_mean[:, i:i + 1], norm.rstd[:, i:i + 1],
                                          ALU.add, ALU.mult)
            last.then_inc(sem(f"{name}_y"), 1)

        ffn_norm = Norm("fn", ln_eps)
        ffn_x_hi = sb("ffn_x_hi", [P, S], F32R)
        ffn_x_lo = sb("ffn_x_lo", [P, S], F32R)
        ffn_s = sb("ffn_s", [P, S])
        ffn_g = sb("ffn_g", [P, S])
        ffn_xb = sb("ffn_xb", [P, 2 * QB, P])

        x_next = sb("x_next", [P, QB, P])
        x_attn = sb("x_attn", [P, QB, P])
        x_ffn = sb("x_ffn", [P, QB, P])
        x_done = sb("x_done", [P, QB, P])

        def seq(b):
            return bass.ds(b * QB, QB)

        def ffn_project_pe(pe, bk, n, before=()):
            wait(pe, f"fn_y", n + 1)
            for s, c in before:
                wait(pe, s, c)
            transposes(pe, bk, ffn_norm.tokens(), QB)\
                .then_inc(sem("f_xt_ps"), 1)

        def ffn_s_pe(pe, bk, n):
            wait(pe, "f_xt_lo", n + 1)
            split_product(pe, bk[:, :], win_hi[:, :], win_lo[:, :], ffn_x_hi[:, :], ffn_x_lo[:, :])\
                .then_inc(sem("f_s_ps"), 1)

        def ffn_out_pe(pe, bk, n):
            wait(pe, "f_add", J * n + J)
            for i in range(QB):
                last = pe.matmul(bk[:, i * P:(i + 1) * P], ffn_g[:, i * P:(i + 1) * P], wout2[:, :],
                                 start=True, stop=True)
            last.then_inc(sem("f_o_ps"), 1)

        def ffn_xhi_act(act, bk, n):
            wait(act, "f_xt_ps", n + 1)
            wait(act, "f_s_ps", n)
            act.copy(ffn_x_hi[:, :], bk[:, :]).then_inc(sem("f_xt_hi"), 1)

        def ffn_xlo_dve(dve, bk, n):
            wait(dve, "f_xt_hi", n + 1)
            dve.tensor_tensor(ffn_x_lo[:, :], bk[:, :], ffn_x_hi[:, :].bitcast(F32), ALU.subtract)\
                .then_inc(sem("f_xt_lo"), 1)

        def ffn_s_act(act, bk, n):
            wait(act, "f_s_ps", n + 1)
            wait(act, "f_relu", J * n)
            act.activation(ffn_s[:, :], bk[:, :], ACT.Identity, bias=bin_2[:, 0:1]).then_inc(sem("f_s"), 1)

        def ffn_relu_act(act, n, j):
            if j == 0:
                wait(act, "f_s", n + 1)
            wait(act, "f_add", J * n + max(j - RELUS + 1, 0))
            act.activation(ffn_relu[:, j % RELUS, :], ffn_s[:, :], ACT.Relu, bias=b1_2[:, j:j + 1],
                           scale=w1_2[:, j:j + 1]).then_inc(sem("f_relu"), 1)

        def ffn_add_dve(dve, n, j):
            wait(dve, "f_relu", J * n + j + 1)
            if j == 0:
                wait(dve, "f_o_ps", n)
                dve.tensor_scalar(ffn_g[:, :], ffn_relu[:, 0, :], w2_2[:, 0:1], b2_2[:, 0:1], ALU.mult, ALU.add)\
                    .then_inc(sem("f_add"), 1)
            else:
                wait(dve, "f_add", J * n + j)
                dve.scalar_tensor_tensor(out=ffn_g[:, :], in0=ffn_relu[:, j % RELUS, :], scalar=w2_2[:, j:j + 1],
                                         in1=ffn_g[:, :], op0=ALU.mult, op1=ALU.add)\
                    .then_inc(sem("f_add"), 1)

        def ffn_xb_pool(pool, n, x_written):
            wait(pool, "f_x2", n - 1)
            wait(pool, *x_written)
            pool.tensor_tensor(ffn_xb[:, bass.ds(n % 2 * QB, QB), :], x_ffn[:, :, :], bout_sb[:, :].unsqueeze(1).broadcast_to([P, QB, P]), ALU.add)\
                .then_inc(sem("f_xb"), 1)

        def ffn_x_dve(dve, bk, n, free=()):
            wait(dve, "f_o_ps", n + 1)
            wait(dve, "f_xb", n + 1)
            wait(dve, "kept", 16 * n)
            for s, c in free:
                wait(dve, s, c)
            dve.tensor_tensor(x_done[:, :, :], bk[:, :].rearrange("p (a d) -> p a d", d=P), ffn_xb[:, bass.ds(n % 2 * QB, QB), :],
                              ALU.add)\
                .then_inc(sem("f_x2"), 1)

        at_norm = Norm("at", ln_eps)
        b_norm = Norm("bn", ln_eps)
        at_x = sb("at_x", [P, S])
        at_x_hi = sb("at_x_hi", [P, S], F32R)
        at_x_lo = sb("at_x_lo", [P, S], F32R)
        at_g_hi = sb("at_g_hi", [P, S], F32R)
        at_g_lo = sb("at_g_lo", [P, S], F32R)
        at_v_hi = sb("at_v_hi", [P, 2 * S], F16)
        at_v_lo = sb("at_v_lo", [P, 2 * S], F16)
        at_neg_max = sb("at_neg_max", [P, QB])
        at_sum = sb("at_sum", [P, QB])
        at_rsum = sb("at_rsum", [P, QB])
        at_scale = sb("at_scale", [P, QB])
        SC, TR, GX, UO, FB = bank[0:3], bank[3:5], bank[5], bank[6], bank[7]

        def v_at(b):
            return b % 2 * S

        def holds(step, first, last):
            return not isinstance(step, int) or first <= step <= last

        def front_parts(b):
            return (holds(b, -2, B - 3), holds(b, -1, B - 2), holds(b, 0, B - 1), holds(b, 1, B),
                    holds(b, 2, B + 1), holds(b, 3, B + 2))

        def front_sync(sp, b):
            if holds(b, 0, B - 1):
                wait(sp, "at_x2", b)
                sp.dma_start(x_attn[:, :, :], x_tiles[:, seq(b), :]).then_inc(sem("x_in"), 16)
            if holds(b, 3, B + 2):
                wait(sp, "f_x2", b - 2)
                sp.dma_start(x_sb[:, seq(b - 3), :], x_done[:, :, :]).then_inc(sem("kept"), 16)
            if holds(b, -3, B - 4):
                wait(sp, "at_y", b + 3)
                sp.dma_start(x_next[:, :, :], x_tiles[:, seq(b + 3), :]).then_inc(sem("x_next_in"), 16)

        def front_tensor(pe, b):
            norm, attn_1, attn_2, ffn_1, ffn_2, turn = front_parts(b)
            if attn_2:
                wait(pe, "at_g_lo", b + 1)
                wait(pe, "at_v_lo", b + 1)
                for u in range(NU):
                    wait(pe, "at_p", NU * (b - 1) + u + 1)
                    if u == 2:
                        wait(pe, "f_s", b - 1)
                    scores(pe, SC[u], u, at_g_hi, at_g_lo, at_x_hi, at_x_lo, 0).then_inc(sem("at_s"), 1)
            if attn_2:
                wait(pe, "at_p", NU * b + 1)
                transposes(pe, TR[0], prob[0], len(unit_blocks(0))).then_inc(sem("at_pt"), 1)
            if attn_1:
                wait(pe, "at_y", b + 2)
                transposes(pe, GX, at_norm.tokens(), QB).then_inc(sem("at_xt_ps"), 1)
            if attn_2:
                wait(pe, "at_p", NU * b + 2)
                transposes(pe, TR[1], prob[1], len(unit_blocks(1))).then_inc(sem("at_pt"), 1)
                wait(pe, "at_p", NU * b + 3)
                wait(pe, "at_pt_lo", NU * b + 1)
                transposes(pe, TR[0], prob[2], len(unit_blocks(2))).then_inc(sem("at_pt"), 1)
            if attn_1:
                wait(pe, "at_x", b + 2)
                wait(pe, "at_p", NU * b + 1)
                for i in range(QB):
                    last = pe.matmul(SC[0][:, i * P:(i + 1) * P], at_x[:, i * P:(i + 1) * P], vo_a[:, :],
                                     start=True, stop=True)
                last.then_inc(sem("at_v_ps"), 1)
                wait(pe, "at_x_lo", b + 2)
                split_product(pe, GX[:, :], qk_a_hi[:, :], qk_a_lo[:, :], at_x_hi[:, :], at_x_lo[:, :])\
                    .then_inc(sem("at_g_ps"), 1)
            for u in range(NU):
                if attn_2:
                    wait(pe, "at_pt_lo", NU * b + u + 1)
                    if u == 0:
                        wait(pe, "at_x2", b)
                    at = v_at(b)
                    weighted_values(pe, lambda i: UO[:, i * P:(i + 1) * P], u,
                                    lambda j: at_v_hi[:, bass.ds(at + j * P, P)],
                                    lambda j: at_v_lo[:, bass.ds(at + j * P, P)])\
                        .then_inc(sem("at_pv"), 1)
                if u == 1 and ffn_1:
                    ffn_project_pe(pe, SC[2], b - 1, before=[("at_p", NU * (b + 1)) if attn_2 else ("f_s", b - 1)])
            if ffn_1:
                ffn_s_pe(pe, SC[2], b - 1)
            if turn:
                wait(pe, "bn_y", b - 2)
                transposes(pe, FB, b_norm.tokens(), QB).then_inc(sem("bn_xt_ps"), 1)
            if ffn_2:
                wait(pe, "bn_xt_lo", b - 2)
                ffn_out_pe(pe, FB, b - 2)

        def front_scalar(act, b):
            norm, attn_1, attn_2, ffn_1, ffn_2, turn = front_parts(b)

            def relus(*js):
                if ffn_2:
                    for j in js:
                        ffn_relu_act(act, b - 2, j)

            def prob_t_scalar(u):
                if attn_2:
                    wait(act, "at_pt", NU * b + u + 1)
                    wait(act, "at_pv", NU * (b - 1) + u + 1)
                    w = len(unit_blocks(u)) * P
                    act.copy(prob_t_hi[u][:, 0:w], TR[u % 2][:, 0:w]).then_inc(sem("at_pt_hi"), 1)

            for u in range(NU):
                relus(u)
                if attn_2:
                    wait(act, "at_m", NU * b + u + 1)
                    if u == 0:
                        wait(act, "at_rsum", b)
                    exponentials(act, SC[u], u, at_neg_max, at_sum).then_inc(sem("at_p"), 1)
            prob_t_scalar(0)
            relus(3)
            if attn_1:
                wait(act, "at_xt_ps", b + 2)
                wait(act, "at_v_ps", b + 1)
                act.copy(at_x[:, :], GX[:, :]).then_inc(sem("at_x"), 1)
                wait(act, "at_s", NU * (b + 1))
                act.copy(at_x_hi[:, :], GX[:, :]).then_inc(sem("at_x_hi"), 1)
            prob_t_scalar(1)
            prob_t_scalar(2)
            relus(4)
            if attn_1:
                wait(act, "at_v_ps", b + 2)
                wait(act, "at_pv", NU * b)
                act.copy(at_v_hi[:, bass.ds(v_at(b + 1), S)], SC[0][:, :]).then_inc(sem("at_v_hi"), 1)
                wait(act, "at_g_ps", b + 2)
                act.copy(at_g_hi[:, :], GX[:, :]).then_inc(sem("at_g_hi"), 1)
            relus(5)
            if ffn_1:
                ffn_xhi_act(act, SC[2], b - 1)
            relus(6)
            if turn:
                wait(act, "bn_xt_ps", b - 2)
                act.copy(yt[:, bass.ds((b - 3) * S, S)], FB[:, :]).then_inc(sem("bn_yt"), 1)
                act.copy(xt_hi[:, bass.ds((b - 3) * S, S)], FB[:, :]).then_inc(sem("bn_xt_hi"), 1)
            relus(7)
            if ffn_1:
                ffn_s_act(act, SC[2], b - 1)

        def front_vector(dve, b):
            norm, attn_1, attn_2, ffn_1, ffn_2, turn = front_parts(b)

            def adds(*js):
                if ffn_2:
                    for j in js:
                        ffn_add_dve(dve, b - 2, j)

            def prob_t_vector(u):
                if attn_2:
                    wait(dve, "at_pt_hi", NU * b + u + 1)
                    w = len(unit_blocks(u)) * P
                    dve.tensor_tensor(prob_t_lo[u][:, 0:w], TR[u % 2][:, 0:w], prob_t_hi[u][:, 0:w], ALU.subtract)\
                        .then_inc(sem("at_pt_lo"), 1)

            for u in range(NU):
                if attn_2:
                    wait(dve, "at_s", NU * b + u + 1)
                    row_maxima(dve, SC[u], u, at_neg_max).then_inc(sem("at_m"), 1)
                adds(u)
                if u == 2 and turn:
                    ffn_x_dve(dve, FB, b - 3, free=[("bn_y", b - 3)])
                    wait(dve, "f_x2", b - 2)
                    norm_statistics(dve, b_norm, lambda i: x_done[:, i, :], b - 3)
            prob_t_vector(0)
            adds(3)
            if attn_1:
                wait(dve, "at_x_hi", b + 2)
                dve.tensor_tensor(at_x_lo[:, :], GX[:, :], at_x_hi[:, :].bitcast(F32), ALU.subtract)\
                    .then_inc(sem("at_x_lo"), 1)
            prob_t_vector(1)
            prob_t_vector(2)
            adds(4)
            if norm:
                wait(dve, "x_next_in", 16 * (b + 3))
                norm_statistics(dve, at_norm, lambda i: x_next[:, i, :], b + 2)
            if attn_1:
                wait(dve, "at_v_hi", b + 2)
                dve.tensor_tensor(at_v_lo[:, bass.ds(v_at(b + 1), S)], SC[0][:, :],
                                  at_v_hi[:, bass.ds(v_at(b + 1), S)], ALU.subtract).then_inc(sem("at_v_lo"), 1)
                wait(dve, "at_g_hi", b + 2)
                dve.tensor_tensor(at_g_lo[:, :], GX[:, :], at_g_hi[:, :].bitcast(F32), ALU.subtract)\
                    .then_inc(sem("at_g_lo"), 1)
            adds(5)
            if ffn_1:
                ffn_xlo_dve(dve, SC[2], b - 1)
            adds(6)
            if turn:
                wait(dve, "bn_xt_hi", b - 2)
                dve.tensor_tensor(xt_lo[:, bass.ds((b - 3) * S, S)], FB[:, :],
                                  xt_hi[:, bass.ds((b - 3) * S, S)].bitcast(F32), ALU.subtract)\
                    .then_inc(sem("bn_xt_lo"), 1)
            adds(7)
            if attn_2:
                wait(dve, "at_p", NU * b + NU)
                dve.reciprocal(at_rsum[:, :], at_sum[:, :]).then_inc(sem("at_rsum"), 1)
                wait(dve, "at_rsum", b + 1)
                dve.tensor_scalar(at_scale[:, :], at_rsum[:, :], scale_up[:, 0:1], None, ALU.mult)\
                    .then_inc(sem("at_scale"), 1)
                wait(dve, "at_scale", b + 1)
                wait(dve, "at_pv", NU * b + NU)
                wait(dve, "x_in", 16 * (b + 1))
                wait(dve, "f_xb", b)
                for i in range(QB):
                    last = dve.scalar_tensor_tensor(out=x_ffn[:, i, :], in0=UO[:, i * P:(i + 1) * P],
                                                    scalar=at_scale[:, i:i + 1], in1=x_attn[:, i, :],
                                                    op0=ALU.mult, op1=ALU.add)
                last.then_inc(sem("at_x2"), 1)
                wait(dve, "at_x2", b + 1)
                norm_statistics(dve, ffn_norm, lambda i: x_ffn[:, i, :], b)

        def front_gpsimd(pool, b):
            norm, attn_1, attn_2, ffn_1, ffn_2, turn = front_parts(b)
            if ffn_1:
                ffn_xb_pool(pool, b - 1, ("at_x2", b))
            if turn:
                norm_apply(pool, b_norm, lambda i: x_done[:, i, :], b - 3, free=[("bn_xt_ps", b - 3)])
            if norm:
                norm_apply(pool, at_norm, lambda i: x_next[:, i, :], b + 2, free=[("at_xt_ps", b + 2)])
            if attn_2:
                norm_apply(pool, ffn_norm, lambda i: x_ffn[:, i, :], b, free=[("f_xt_ps", b)])

        NS = 2 * NU
        staging = ExitStack()

        def staged(name, shape):
            return staging.enter_context(nc.sbuf_tensor(name, shape, F32))

        wq_a = staged("wq_a", [P, OC, P])
        wk_a = staged("wk_a", [P, OC, P])
        wv_a = staged("wv_a", [P, OC, P])
        wo_a = staged("wo_a", [P, O])
        wq_b = staged("wq_b", [P, H, E])
        wk_b = staged("wk_b", [P, H, E])
        wv_b = staged("wv_b", [P, H, E])
        wo_b = staged("wo_b", [P, HP, P])
        wo_a_t = staged("wo_a_t", [P, OC, P])
        wq_b_t = staged("wq_b_t", [P, HP, P])
        wk_b_t = staged("wk_b_t", [P, HP, P])
        qk_b = staged("qk_b", [P, H, P])
        staging.close()

        LOADED_QK_A, LOADED_A, LOADED_B, LOADED_F = "load_qk_a", "load_a", "load_b", "load_f"
        a_loads = [(wq_a[:, :, :], a_wq.rearrange("(c p) i -> p c i", p=P)),
                   (wk_a[:, :, :], a_wk.rearrange("(c p) i -> p c i", p=P)),
                   (wo_a[:, :], a_wo),
                   (wv_a[:, :, :], a_wv.rearrange("(c p) i -> p c i", p=P))]
        b_loads = [(wq_b[:, :, :], b_wq.rearrange("h d e -> d h e")),
                   (wk_b[:, :, :], b_wk.rearrange("h d e -> d h e")),
                   (wv_b[:, :, :], b_wv.rearrange("h d e -> d h e")),
                   (wo_b[:, :, :], b_wo.rearrange("(c p) d -> p c d", p=P))]
        f_loads = [(win2[:, 0, :], f_win), (win2[:, 1, :], f_win),
                   (wout2[0:M, :], f_wout), (wout2[M:P, :], f_wout),
                   (w1_2[0:M, :], f_w1[:, 0:J]), (w1_2[M:P, :], f_w1[:, J:INNER]),
                   (b1_2[0:M, :], f_b1[:, 0:J]), (b1_2[M:P, :], f_b1[:, J:INNER]),
                   (w2_2[0:M, :], f_w2[:, 0:J]), (w2_2[M:P, :], f_w2[:, J:INNER]),
                   (bin_2[0:M, :], f_bin.rearrange("(m o) -> m o", o=1)),
                   (bin_2[M:P, :], f_bin.rearrange("(m o) -> m o", o=1)),
                   (b2_2[0:M, :], f_b2.rearrange("(m o) -> m o", o=1)),
                   (gamma_sb[:, :], gamma.rearrange("(o d) -> o d", o=1).broadcast_to([P, P])),
                   (beta_sb[:, :], beta.rearrange("(o d) -> o d", o=1).broadcast_to([P, P])),
                   (bout_sb[:, :], f_bout.rearrange("(o d) -> o d", o=1).broadcast_to([P, P]))]
        x_tiles = x_in.rearrange("b (n p) d -> p (b n) d", p=P)
        out_tiles = out.rearrange("b (n p) d -> p (b n) d", p=P)
        ALL_B, ALL_F = 16 * len(b_loads), 16 * len(f_loads)

        qk_now = [sb(f"qk_now{h}", [P, 2, P], F32R) for h in range(2)]
        wo_now = sb("wo_now", [P, 2, P], F32R)
        xv_now = sb("xv_now", [P, 2, P], F32R)
        g_hi = [at_g_hi, sb("g_hi1", [P, S], F32R)]
        g_lo = [at_g_lo, sb("g_lo1", [P, S], F32R)]
        v_hi = sb("v_hi", [P, SLOTS * QB * P], F16)
        v_lo = sb("v_lo", [P, SLOTS * QB * P], F16)
        RELUS = 4
        ffn_relu = v_hi[:, 0:2 * RELUS * S].bitcast(F32).rearrange("p (r t) -> p r t", t=S)
        neg_max = sb("neg_max", [P, 2, QB])
        sums = sb("sums", [P, 2, QB])
        rsum = sb("rsum", [P, 2, QB])
        ctx_sb = sb("ctx_sb", [P, QB, 2, E])
        ctx_t_hi, ctx_t_lo = at_x_hi, at_x_lo
        CT, GB, MB = bank[5], bank[6], bank[7]
        VB = [MB, CT, SC[0], SC[1]]
        VSLICES = 2 * QB

        def lagged(t, s, lag):
            return (t, s - lag) if s >= lag else (t - 1, s - lag + NS)

        def exists(t):
            return not isinstance(t, int) or t >= 0

        def x_at(t):
            return t // HP * S

        def v_slot_at(t):
            return t % SLOTS * (QB * P)

        def v_dst(buf, k):
            whole = buf[:, :].rearrange("p (s r) -> p s r", r=QB * P)
            slot = k // VSLICES % 2 * HP + k % 2 * (HP // 2)
            return whole[:, bass.ds(slot, HP // 2), bass.ds(k % VSLICES // 2 * P, P)]

        def raw(ap):
            return ap.bitcast(F32)

        def keys_sync(sp, t, h):
            sp.dma_start(raw(qk_now[h][:, :, :]), raw(qk_b_parts[:, bass.ds((2 * t + h) % H, 1), :, :]))\
                .then_inc(sem(f"qk_in{h}"), 16)

        def first_values_tensor(pe, k):
            wait(pe, "v_lo", k - len(VB) + 1)
            x = slice(k // 2 * P, (k // 2 + 1) * P)
            half = slice(k % 2 * 512, (k % 2 + 1) * 512)
            split_product(pe, VB[k % len(VB)][:, :], xt_hi[:, x], xt_lo[:, x], wv_b_hi[:, half], wv_b_lo[:, half])\
                .then_inc(sem("v_ps"), 1)

        def values_sync(sp, k):
            wait(sp, "v_ps", k)
            at = k // 2 * P
            sp.dma_start(raw(xv_now[:, 0, :]), raw(xt_hi[:, bass.ds(at, P)])).then_inc(sem("xv_in"), 16)
            sp.dma_start(raw(xv_now[:, 1, :]), raw(xt_lo[:, bass.ds(at, P)])).then_inc(sem("xv_in"), 16)

        def values_tensor(pe, k, busy):
            wait(pe, "xv_in", 32 * (k + 1 - VSLICES))
            wait(pe, *busy)
            half = bass.ds(k % 2 * 512, 512)
            split_product(pe, MB[:, :], xv_now[:, 0, :], xv_now[:, 1, :], wv_b_hi[:, half], wv_b_lo[:, half])\
                .then_inc(sem("v_ps"), 1)

        def values_scalar(act, k, bk=MB):
            wait(act, "v_ps", k + 1)
            act.copy(v_dst(v_hi, k), bk[:, :].rearrange("p (s c) -> p s c", c=P)).then_inc(sem("v_hi"), 1)

        def values_vector(dve, k, bk=MB):
            wait(dve, "v_hi", k + 1)
            dve.tensor_tensor(v_dst(v_lo, k), bk[:, :].rearrange("p (s c) -> p s c", c=P), v_dst(v_hi, k),
                              ALU.subtract).then_inc(sem("v_lo"), 1)

        def keys_tensor(pe, t, h):
            wait(pe, f"qk_in{h}", 16 * (t + 1))
            if h == 0:
                wait(pe, "g_lo1", t)
            else:
                wait(pe, "g_lo0", t + 1)
            split_product(pe, GB[:, :], qk_now[h][:, 0, :], qk_now[h][:, 1, :],
                          xt_hi[:, bass.ds(x_at(t), S)], xt_lo[:, bass.ds(x_at(t), S)])\
                .then_inc(sem(f"g_ps{h}"), 1)

        def keys_scalar(act, t, h):
            wait(act, f"g_ps{h}", t + 1)
            act.copy(g_hi[h][:, :], GB[:, :]).then_inc(sem(f"g_hi{h}"), 1)

        def keys_vector(dve, t, h):
            wait(dve, f"g_hi{h}", t + 1)
            dve.tensor_tensor(g_lo[h][:, :], GB[:, :], g_hi[h][:, :].bitcast(F32), ALU.subtract)\
                .then_inc(sem(f"g_lo{h}"), 1)

        def heads_tensor(pe, t, fresh=True, vslice=True, next_pair=True):
            for s in range(NS):
                u, h = s % NU, s // NU
                t2, s2 = lagged(t, s, 2)
                t3, s3 = lagged(t, s, 3)
                t4, s4 = lagged(t, s, 4)
                if fresh:
                    if u == 0:
                        wait(pe, f"g_lo{h}", t + 1)
                    if exists(t3):
                        wait(pe, f"p{s3}", t3 + 1)
                    scores(pe, SC[u], u, g_hi[h], g_lo[h], xt_hi, xt_lo, x_at(t)).then_inc(sem(f"s{s}"), 1)
                if exists(t2) and (fresh or s < 2):
                    wait(pe, f"p{s2}", t2 + 1)
                    if exists(t4):
                        wait(pe, f"pt_lo{s4}", t4 + 1)
                    transposes(pe, TR[s2 % 2], prob[s2 % NU], len(unit_blocks(s2 % NU)))\
                        .then_inc(sem(f"pt{s2}"), 1)
                if exists(t3) and (fresh or s < 3):
                    if s3 == 0:
                        wait(pe, "ctx", t3)
                        wait(pe, "v_lo", t3 // HP * VSLICES + VSLICES)
                    wait(pe, f"pt_lo{s3}", t3 + 1)
                    h3 = s3 // NU
                    at = v_slot_at(t3)
                    weighted_values(pe, lambda i: CT[:, i * P + h3 * E:i * P + (h3 + 1) * E], s3 % NU,
                                    lambda j: v_hi[:, bass.ds(at + (j * P + h3 * E), E)],
                                    lambda j: v_lo[:, bass.ds(at + (j * P + h3 * E), E)])\
                        .then_inc(sem(f"pv{s3}"), 1)
                if s == 0 and fresh:
                    keys_tensor(pe, t, 1)
                if s == 1 and vslice:
                    values_tensor(pe, t + VSLICES, ("y_acc", t - 1))
                if s == 2 and next_pair:
                    keys_tensor(pe, t + 1, 0)
                if s == 3 and exists(t - 1):
                    wait(pe, "ctx", t)
                    if vslice:
                        wait(pe, "v_lo", t + VSLICES + 1)
                    else:
                        wait(pe, "y_acc", t - 1)
                    transposes(pe, MB, ctx_sb[:, :, :, :].rearrange("p a h e -> p (a h e)"), QB)\
                        .then_inc(sem("ctx_t_ps"), 1)
                if s == 5 and exists(t - 1):
                    wait(pe, "wo_in", 16 * t)
                    wait(pe, "ctx_t_lo", t)
                    split_product(pe, MB[:, :], wo_now[:, 0, :], wo_now[:, 1, :], ctx_t_hi[:, :], ctx_t_lo[:, :])\
                        .then_inc(sem("y_ps"), 1)

        def heads_scalar(act, t, fresh=True, vslice=True, next_pair=True):
            for s in range(NS):
                u, h = s % NU, s // NU
                t2, s2 = lagged(t, s, 2)
                t3, s3 = lagged(t, s, 3)
                t5, s5 = lagged(t, s, 5)
                if s == 1 and fresh:
                    keys_scalar(act, t, 1)
                if s == 2 and vslice:
                    wait(act, "pv5", t - 1)
                    values_scalar(act, t + VSLICES)
                if s == 3 and next_pair:
                    keys_scalar(act, t + 1, 0)
                if s == 4 and exists(t - 1):
                    wait(act, "ctx_t_ps", t)
                    wait(act, "y_ps", t - 1)
                    act.copy(ctx_t_hi[:, :], MB[:, :]).then_inc(sem("ctx_t_hi"), 1)
                if exists(t2) and (fresh or s < 2):
                    wait(act, f"pt{s2}", t2 + 1)
                    if exists(t5):
                        wait(act, f"pv{s5}", t5 + 1)
                    w = len(unit_blocks(s2 % NU)) * P
                    act.copy(prob_t_hi[s2 % NU][:, 0:w], TR[s2 % 2][:, 0:w]).then_inc(sem(f"pt_hi{s2}"), 1)
                if fresh:
                    wait(act, f"m{s}", t + 1)
                    if exists(t3):
                        wait(act, f"pt{s3}", t3 + 1)
                    if u == 0:
                        wait(act, f"rsum{h}", t)
                    exponentials(act, SC[u], u, neg_max[:, h, :], sums[:, h, :]).then_inc(sem(f"p{s}"), 1)

        def heads_vector(dve, t, fresh=True, vslice=True, next_pair=True):
            for s in range(NS):
                u, h = s % NU, s // NU
                t2, s2 = lagged(t, s, 2)
                if fresh:
                    wait(dve, f"s{s}", t + 1)
                    row_maxima(dve, SC[u], u, neg_max[:, h, :]).then_inc(sem(f"m{s}"), 1)
                if exists(t2) and (fresh or s < 2):
                    wait(dve, f"pt_hi{s2}", t2 + 1)
                    w = len(unit_blocks(s2 % NU)) * P
                    dve.tensor_tensor(prob_t_lo[s2 % NU][:, 0:w], TR[s2 % 2][:, 0:w], prob_t_hi[s2 % NU][:, 0:w],
                                      ALU.subtract).then_inc(sem(f"pt_lo{s2}"), 1)
                if s == 0 and exists(t - 2):
                    output_vector(dve, t - 2)
                if s == 0 and exists(t - 1):
                    wait(dve, "p5", t)
                    dve.reciprocal(rsum[:, 1, :], sums[:, 1, :]).then_inc(sem("rsum1"), 1)
                if s == 1 and fresh:
                    keys_vector(dve, t, 1)
                if s == 2 and exists(t - 1):
                    wait(dve, "pv5", t)
                    wait(dve, "rsum1", t)
                    wait(dve, "ctx_t_ps", t - 1)
                    dve.tensor_tensor(ctx_sb[:, :, :, :], CT[:, :].rearrange("p (a h e) -> p a h e", h=2, e=E),
                                      rsum[:, :, :].rearrange("p h a -> p a h").unsqueeze(3)
                                      .broadcast_to([P, QB, 2, E]), ALU.mult).then_inc(sem("ctx"), 1)
                if s == 2 and vslice:
                    values_vector(dve, t + VSLICES)
                if s == 3 and next_pair:
                    keys_vector(dve, t + 1, 0)
                if s == 3 and fresh:
                    wait(dve, "p2", t + 1)
                    wait(dve, "ctx", t)
                    dve.reciprocal(rsum[:, 0, :], sums[:, 0, :]).then_inc(sem("rsum0"), 1)
                if s == 4 and exists(t - 1):
                    wait(dve, "ctx_t_hi", t)
                    dve.tensor_tensor(ctx_t_lo[:, :], MB[:, :], ctx_t_hi[:, :].bitcast(F32), ALU.subtract)\
                        .then_inc(sem("ctx_t_lo"), 1)

        def output_vector(dve, t):
            wait(dve, "y_ps", t + 1)
            at = bass.ds(x_at(t), S)
            dve.tensor_tensor(yt[:, at], MB[:, :], yt[:, at], ALU.add).then_inc(sem("y_acc"), 1)

        y_norm = Norm("yn", ln_b_eps)
        y_now, y_tok, y_gb = at_x, at_norm.y, b_norm.y
        x_beta = sb("x_beta", [P, QB, P])
        YB, FK, FP = bank[0], bank[1], bank[2]

        def back_sync(sp, b):
            if holds(b, 0, B - 1):
                wait(sp, "x_beta", b)
                wait(sp, "kept", 16 * B)
                sp.dma_start(x_attn[:, :, :], x_sb[:, seq(b), :]).then_inc(sem("x_in"), 16)
            if holds(b, 3, B + 2):
                wait(sp, "f_x2", B + b - 2)
                sp.dma_start(out_tiles[:, seq(b - 3), :], x_done[:, :, :]).then_inc(sem("kept"), 16)

        def y_turn_tensor(pe, b):
            wait(pe, "y_now", b + 1)
            wait(pe, "y_tok", b)
            transposes(pe, YB, y_now, QB).then_inc(sem("y_tok_ps"), 1)

        def back_tensor(pe, b):
            r = B + b - 2
            if holds(b, 0, B - 2):
                y_turn_tensor(pe, b + 1)
            if holds(b, 1, B):
                ffn_project_pe(pe, FP, r + 1, before=[("f_s", r + 1)])
            if holds(b, 1, B):
                ffn_s_pe(pe, FP, r + 1)
            if holds(b, 2, B + 1):
                wait(pe, "f_x2", r)
                ffn_out_pe(pe, FK, r)

        def back_scalar(act, b):
            r = B + b - 2
            for j in range(J):
                if holds(b, 2, B + 1):
                    ffn_relu_act(act, r, j)
                if j == J // 2:
                    if holds(b, 0, B - 2):
                        y_tok_scalar(act, b + 1)
                    if holds(b, 0, B - 3):
                        y_now_scalar(act, b + 2)
            if holds(b, 1, B):
                ffn_xhi_act(act, FP, r + 1)
                ffn_s_act(act, FP, r + 1)

        def y_now_scalar(act, b):
            wait(act, "y_tok_ps", b)
            act.copy(y_now[:, :], yt[:, bass.ds(b * S, S)]).then_inc(sem("y_now"), 1)

        def y_tok_scalar(act, b):
            wait(act, "y_tok_ps", b + 1)
            wait(act, "yn_y", b)
            act.copy(y_tok[:, :, :], YB[:, :]).then_inc(sem("y_tok"), 1)

        def back_vector(dve, b):
            r = B + b - 2

            def adds(*js):
                if holds(b, 2, B + 1):
                    for j in js:
                        ffn_add_dve(dve, r, j)

            if holds(b, 1, B):
                wait(dve, "yn_y", b)
                dve.tensor_tensor(y_gb[:, :, :], y_norm.y[:, :, :],
                                  gamma_sb[:, :].unsqueeze(1).broadcast_to([P, QB, P]), ALU.mult)\
                    .then_inc(sem("y_gb"), 1)
            if holds(b, 0, B - 1):
                wait(dve, "y_tok", b + 1)
                norm_statistics(dve, y_norm, lambda i: y_tok[:, i, :], b)
            adds(0)
            if holds(b, 1, B):
                wait(dve, "y_gb", b)
                wait(dve, "x_beta", b)
                wait(dve, "f_xb", B + b - 1)
                dve.tensor_tensor(x_ffn[:, :, :], y_gb[:, :, :], x_beta[:, :, :], ALU.add).then_inc(sem("y_x2"), 1)
            adds(1)
            if holds(b, 1, B):
                wait(dve, "y_x2", b)
                norm_statistics(dve, ffn_norm, lambda i: x_ffn[:, i, :], r + 1)
            adds(2)
            if holds(b, 3, B + 2):
                ffn_x_dve(dve, FK, r - 1)
            adds(3, 4, 5, 6, 7)
            if holds(b, 1, B):
                ffn_xlo_dve(dve, FP, r + 1)

        def back_gpsimd(pool, b):
            r = B + b - 2
            if holds(b, 0, B - 1):
                norm_apply(pool, y_norm, lambda i: y_tok[:, i, :], b, free=[("y_gb", b)])
            if holds(b, 1, B):
                norm_apply(pool, ffn_norm, lambda i: x_ffn[:, i, :], r + 1, free=[("f_xt_ps", r + 1)])
            if holds(b, 0, B - 1):
                wait(pool, "y_x2", b)
                wait(pool, "x_in", 16 * (B + b + 1))
                pool.tensor_tensor(x_beta[:, :, :], x_attn[:, :, :], beta_sb[:, :].unsqueeze(1).broadcast_to([P, QB, P]),
                                   ALU.add).then_inc(sem("x_beta"), 1)
            if holds(b, 1, B):
                ffn_xb_pool(pool, r + 1, ("y_x2", b))

        block = ctx.enter_context(nc.Block())

        def over_steps(eng, body, first, loop, last):
            for b in range(first, loop[0]):
                body(eng, b)
            with eng.Fori(*loop) as b:
                body(eng, b)
            for b in range(loop[1], last + 1):
                body(eng, b)

        def over_front(eng, body):
            over_steps(eng, body, -1, (4, B - 2), B + 2)

        def over_back(eng, body):
            over_steps(eng, body, 0, (3, B - 2), B + 2)

        def over_pairs(eng, body):
            body(eng, 0)
            body(eng, 1)
            with eng.Fori(2, PAIRS - HP) as t:
                body(eng, t)
            with eng.Fori(PAIRS - HP, PAIRS - 1) as t:
                body(eng, t, vslice=False)
            body(eng, PAIRS - 1, vslice=False, next_pair=False)

        @block.sync
        def _(sp):
            front_sync(sp, -3)
            prepare_loads_sync(sp)
            over_steps(sp, front_sync, -2, (3, B - 3), B + 2)
            sp.wait_ge(sem("qk_b_lo"), 4)
            for h in range(2):
                keys_sync(sp, 0, h)
            sp.wait_ge(sem("wo_b_lo"), 1)
            wait(sp, "bn_xt_lo", B)
            wait(sp, "g_ps0", 1)
            keys_sync(sp, 1, 0)
            values_sync(sp, VSLICES)

            def body(sp, t, vslice=True):
                if holds(t, 0, PAIRS - 2):
                    wait(sp, "g_ps1", t + 1)
                    keys_sync(sp, t + 1, 1)
                if vslice:
                    values_sync(sp, t + 1 + VSLICES)
                if holds(t, 0, PAIRS - 3):
                    wait(sp, "g_ps0", t + 2)
                    keys_sync(sp, t + 2, 0)
                wait(sp, "y_ps", t)
                sp.dma_start(raw(wo_now[:, :, :]), raw(wo_b_parts[:, bass.ds(t % HP, 1), :, :]))\
                    .then_inc(sem("wo_in"), 16)

            body(sp, 0)
            with sp.Fori(1, PAIRS - HP - 1) as t:
                body(sp, t, vslice=True)
            with sp.Fori(PAIRS - HP - 1, PAIRS - 2) as t:
                body(sp, t, vslice=False)
            for t in (PAIRS - 2, PAIRS - 1):
                body(sp, t, vslice=False)
            over_back(sp, back_sync)
            sp.wait_ge(sem("kept"), 16 * 2 * B)

        @block.gpsimd
        def _(pool):
            prepare_gpsimd(pool)
            pool.wait_ge(sem(LOADED_F), ALL_F)
            over_front(pool, front_gpsimd)
            over_back(pool, back_gpsimd)

        @block.tensor
        def _(pe):
            prepare_tensor(pe)
            pe.wait_ge(sem("qk_a_lo"), 1)
            pe.wait_ge(sem("vo_a"), 1)
            pe.wait_ge(sem("win_lo"), 1)
            pe.wait_ge(sem("qk_b_hi"), 4)
            over_front(pe, front_tensor)
            pe.wait_ge(sem("wv_b_lo"), 1)
            pe.wait_ge(sem("bn_xt_lo"), B)
            for k in range(VSLICES):
                first_values_tensor(pe, k)
            keys_tensor(pe, 0, 0)
            pe.wait_ge(sem("v_lo"), VSLICES)
            over_pairs(pe, heads_tensor)
            heads_tensor(pe, PAIRS, fresh=False, vslice=False, next_pair=False)
            y_turn_tensor(pe, 0)
            over_back(pe, back_tensor)

        @block.scalar
        def _(act):
            prepare_loads_scalar(act)
            prepare_scalar(act)
            over_front(act, front_scalar)
            for k in range(VSLICES):
                values_scalar(act, k, VB[k % len(VB)])
            keys_scalar(act, 0, 0)
            over_pairs(act, heads_scalar)
            heads_scalar(act, PAIRS, fresh=False, vslice=False, next_pair=False)
            act.wait_ge(sem("y_acc"), PAIRS)
            y_now_scalar(act, 0)
            y_tok_scalar(act, 0)
            y_now_scalar(act, 1)
            over_back(act, back_scalar)

        @block.vector
        def _(dve):
            front_vector(dve, -2)
            prepare_vector(dve)
            over_front(dve, front_vector)
            for k in range(VSLICES):
                values_vector(dve, k, VB[k % len(VB)])
            keys_vector(dve, 0, 0)
            over_pairs(dve, heads_vector)
            heads_vector(dve, PAIRS, fresh=False, vslice=False, next_pair=False)
            output_vector(dve, PAIRS - 1)
            over_back(dve, back_vector)


_INS = ['L0_attn_a_in_features', 'L0_attn_a_w_q', 'L0_attn_a_w_k', 'L0_attn_a_w_v', 'L0_attn_a_w_o',
        'L0_attn_b_Wq', 'L0_attn_b_Wk', 'L0_attn_b_Wv', 'L0_attn_b_Wo', 'L0_attn_b_gamma', 'L0_attn_b_beta',
        'L0_ffn_Win', 'L0_ffn_bin_', 'L0_ffn_W1', 'L0_ffn_b1', 'L0_ffn_W2', 'L0_ffn_b2', 'L0_ffn_Wout',
        'L0_ffn_bout']


def kernel(**inputs):
    import numpy as np
    import concourse.bacc as bacc
    from concourse.bass_utils import run_bass_kernel_spmd

    nc = bacc.Bacc("TRN2", target_bir_lowering=False, num_devices=1)
    arrays, args = {}, []
    for name in _INS:
        a = np.ascontiguousarray(inputs[name])
        arrays[f"in_{name}"] = a
        args.append(nc.dram_tensor(f"in_{name}", a.shape, mybir.dt.from_np(a.dtype), kind="ExternalInput").ap())
    shape = inputs[_INS[0]].shape
    args.append(nc.dram_tensor("out_x", shape, F32, kind="ExternalOutput").ap())
    hybrid_kernel(nc, *args)
    r = run_bass_kernel_spmd(nc, [arrays], core_ids=[0])
    return r.results[0]["out_x"]
```
